# Optimizing a Trainium2 kernel written in Bass

```python
import numpy as np
import jax
import jax.numpy as jnp

def _softmax(x, axis=-1):
    return jax.nn.softmax(x, axis=axis)

def _gelu(x):
    return jax.nn.gelu(x, approximate=True)

def _silu(x):
    return jax.nn.silu(x)

def _sigmoid(x):
    return jax.nn.sigmoid(x)

def _layernorm(x, axis=-1, eps=1e-05):
    m = jnp.mean(x, axis=axis, keepdims=True)
    v = jnp.var(x, axis=axis, keepdims=True)
    return (x - m) / jnp.sqrt(v + eps)

def _scatter_add(tgt, idx, src, axis=0):
    return tgt.at[idx].add(src)

def _segment_sum(src, seg, n):
    return jax.ops.segment_sum(src, seg, n)
kernel_name = 'mk_gnn_ffn_d1_gnn_r8_b538a9'

def setup_inputs(seed: int=0):
    np.random.seed(seed)
    _w = jnp.asarray

    def _rec_inputs():
        import jax
        import jax.numpy as jnp
        _gk = jax.random.key(seed)
        x = -6.415e-05 + 1 * jax.random.normal(jax.random.fold_in(_gk, 1), (2500, 512), jnp.float32)
        src = jax.random.randint(jax.random.fold_in(_gk, 2), (80000,), 0, 2500, jnp.int32)
        dst = jax.random.randint(jax.random.fold_in(_gk, 3), (80000,), 0, 2500, jnp.int32)
        _o = jnp.argsort(dst, stable=True)
        src = src[_o]
        dst = dst[_o]
        return (x, src, dst)
    x, src, dst = _rec_inputs()

    def _L0_gnn_setup():
        import jax, jax.numpy as jnp
        import numpy as np
        N_NODES = 2500
        key = jax.random.key(seed)
        ks = jax.random.split(key, 6)
        d = 512
        E = 80000
        x = jax.random.normal(ks[0], (N_NODES, d), dtype=jnp.float32)
        edge_index = jax.random.randint(ks[1], (2, E), 0, N_NODES, dtype=jnp.int64)
        s = 1.0 / np.sqrt(d)
        W1 = jax.random.uniform(ks[2], (d, d), jnp.float32, -s, s)
        b1 = jax.random.uniform(ks[3], (d,), jnp.float32, -s, s)
        W2 = jax.random.uniform(ks[4], (d, d), jnp.float32, -s, s)
        b2 = jax.random.uniform(ks[5], (d,), jnp.float32, -s, s)
        return {'x': x, 'edge_index': edge_index, 'W1': W1, 'b1': b1, 'W2': W2, 'b2': b2}
    _L0_gnn_all = _L0_gnn_setup()
    _L0_gnn_in = {k: v for k, v in _L0_gnn_all.items() if k in ('W1', 'b1', 'W2', 'b2')}
    del _L0_gnn_all

    def _L0_ffn_setup():
        import jax, jax.numpy as jnp
        import numpy as np
        B, L, D, H, E, K = (8, 1024, 512, 256, 8, 2)
        SCALE = 0.02
        key = jax.random.key(seed)
        ks = jax.random.split(key, 6)
        return {'x': jax.random.normal(ks[0], (B, L, D), dtype=jnp.float32), 'Wg': jax.random.normal(ks[1], (D, E), dtype=jnp.float32) * SCALE, 'W1': jax.random.normal(ks[2], (E, D, H), dtype=jnp.float32) * SCALE, 'b1': jax.random.normal(ks[3], (E, H), dtype=jnp.float32) * SCALE, 'W2': jax.random.normal(ks[4], (E, H, D), dtype=jnp.float32) * SCALE, 'b2': jax.random.normal(ks[5], (E, D), dtype=jnp.float32) * SCALE}
    _L0_ffn_all = _L0_ffn_setup()
    _L0_ffn_in = {k: v for k, v in _L0_ffn_all.items() if k in ('Wg', 'W1', 'b1', 'W2', 'b2')}
    del _L0_ffn_all
    return {'x': x, 'src': src, 'dst': dst, 'L0_gnn_W1': _L0_gnn_in['W1'], 'L0_gnn_b1': _L0_gnn_in['b1'], 'L0_gnn_W2': _L0_gnn_in['W2'], 'L0_gnn_b2': _L0_gnn_in['b2'], 'L0_ffn_Wg': _L0_ffn_in['Wg'], 'L0_ffn_W1': _L0_ffn_in['W1'], 'L0_ffn_b1': _L0_ffn_in['b1'], 'L0_ffn_W2': _L0_ffn_in['W2'], 'L0_ffn_b2': _L0_ffn_in['b2']}

def reference(x, src, dst, L0_gnn_W1, L0_gnn_b1, L0_gnn_W2, L0_gnn_b2, L0_ffn_Wg, L0_ffn_W1, L0_ffn_b1, L0_ffn_W2, L0_ffn_b2):
    import jax
    import jax.numpy as jnp

    def _L0_gnn_ref(x, edge_index, W1, b1, W2, b2):
        import jax, jax.numpy as jnp
        import numpy as np
        N_NODES = 2500
        eps = 0.0
        src, dst = (edge_index[0], edge_index[1])
        agg = jax.ops.segment_sum(x[src], dst, num_segments=N_NODES)
        h = (1.0 + eps) * x + agg
        h = jax.nn.relu(h @ W1 + b1)
        out = h @ W2 + b2
        return out

    def _L0_ffn_ref(x, Wg, W1, b1, W2, b2):
        import jax, jax.numpy as jnp
        import numpy as np
        B, L, D, H, E, K = (8, 1024, 512, 256, 8, 2)
        SCALE = 0.02
        b, l, d = x.shape
        xt = x.reshape(-1, d)
        T = xt.shape[0]
        gate = jax.nn.softmax(xt @ Wg, axis=-1)
        topv, topi = jax.lax.top_k(gate, K)
        topv = topv / (jnp.sum(topv, axis=-1, keepdims=True) + 1e-06)
        scores = jnp.zeros((T, E), dtype=xt.dtype).at[jnp.arange(T)[:, None], topi].set(topv)
        out = jnp.zeros_like(xt)
        for e in range(E):
            h = jax.nn.gelu(xt @ W1[e] + b1[e], approximate=False)
            ye = h @ W2[e] + b2[e]
            out = out + ye * scores[:, e:e + 1]
        return out.reshape(b, l, d)
    edge_index = jnp.stack([src, dst])
    x = x + _L0_gnn_ref(_layernorm(x, axis=-1), edge_index, L0_gnn_W1, L0_gnn_b1, L0_gnn_W2, L0_gnn_b2)
    x = x + _L0_ffn_ref(_layernorm(x, axis=-1)[None], L0_ffn_Wg, L0_ffn_W1, L0_ffn_b1, L0_ffn_W2, L0_ffn_b2)[0]
    return x

_drawn_inputs = setup_inputs


def setup_inputs(seed=0):
    import zlib

    import numpy as np

    out = dict(_drawn_inputs(seed))
    spreads = {}
    factors = {'L0_gnn_b1': 8.0, 'L0_gnn_b2': 3.601, 'L0_ffn_b1': 36.336, 'L0_ffn_b2': 6.562}
    for name, (base, spread) in spreads.items():
        noise = np.random.default_rng([zlib.crc32(name.encode()), seed]).standard_normal(out[name].shape)
        drawn = base * np.exp(spread * noise) if base else spread * noise
        out[name] = jnp.asarray(drawn.astype(out[name].dtype))
    for name, factor in factors.items():
        out[name] = (out[name] * factor).astype(out[name].dtype)
    return out
```

```python
from contextlib import ExitStack

import concourse.bass as bass
from concourse import mybir

F32 = mybir.dt.float32
F32R = mybir.dt.float32r
F16 = mybir.dt.float16
BF16 = mybir.dt.bfloat16
I32 = mybir.dt.int32
U32 = mybir.dt.uint32
ALU = mybir.AluOpType
ACT = mybir.ActivationFunctionType
AX = mybir.AxisListType

N, D, E = 2500, 512, 80000
P = 125
T = N // P
KC = D // 128
CH = 128
NCH = E // CH
CPP = NCH // P
W = 20
NW = N // W
MW = W * T
KS = 7
FULL = 255
KP = 8
ROWS = 640
G = 5
GN = N // G
WG = NW // G
PARTS = 5
WP = WG // PARTS
TP = T // PARTS
LOOK = 6
RING = 4
NE, H, HC = 8, 256, 2
FAR = -1.0e6
EPS = 1e-5
ROUND = 12582912.0


def gnn_moe(nc, x, src, dst, gW1, gb1, gW2, gb2, Wg, eW1, eb1, eW2, eb2, out):
    ctx = ExitStack()
    with ctx:
        def sem(name):
            return ctx.enter_context(nc.semaphore(name))

        def allocator(stack):
            return lambda name, shape, dt: stack.enter_context(nc.sbuf_tensor(name, shape, dt))

        edge_rows = nc.dram_tensor("edge_rows", [ROWS, 2 * CH], F32).ap()
        spans_d = nc.dram_tensor("spans_d", [2, NCH], F32).ap()
        x2_d = nc.dram_tensor("x2_d", [N, D], F32).ap()
        xt_d = nc.dram_tensor("xt_d", [N, D], F32).ap()
        range_d = nc.dram_tensor("range_d", [1, 2 * NW + 1], I32).ap()
        counts_d = nc.dram_tensor("counts_d", [2, 128, T, N], BF16).ap()

        keep = allocator(ctx)
        eps_t = keep("eps_t", [128, 1], F32)
        ident = keep("ident", [128, 128], F32)
        ones = keep("ones", [P, 1], F32)
        flag_i = keep("flag_i", [1, 1], I32)
        range_row = keep("range_row", [1, 2 * NW + 1], I32)
        iota_e = keep("iota_e", [P, NE], F32)

        graph = ExitStack()
        sb = allocator(graph)
        xn_hi = sb("xn_hi", [P, T, D], F16)
        xn_lo = sb("xn_lo", [P, T, D], F16)
        general = ExitStack()
        gb = allocator(general)
        key_all = gb("key_all", [128, ROWS], F32)
        lo_all = gb("lo_all", [128, ROWS], F32)
        gen_key = gb("gen_key", [128, MW], F16)
        gen_lo = gb("gen_lo", [128, 128], F16)
        gen_counts = gb("gen_counts", [128, 2, T, W], BF16)
        general.close()
        counts = sb("counts", [128, 2, T, GN], BF16)
        gather = ExitStack()
        slot_rows = allocator(gather)("slot_rows", [NW, KS, 2 * CH], F32)
        dst_next = allocator(gather)("dst_next", [P, 2, CPP * CH], I32)
        gather.close()
        hot_key = sb("hot_key", [128, RING, KS, MW], F16)
        hot_lo = sb("hot_lo", [128, RING, 128, KP], F16)
        W1_hi, W1_lo, W2_hi, W2_lo = (sb(n, [128, KC, D], F32R) for n in ("W1_hi", "W1_lo", "W2_hi", "W2_lo"))
        b1_col = sb("b1_col", [128, KC], F32)
        b2_row = sb("b2_row", [P, D], F32)
        key_w = sb("key_w", [128, KS, NW], F32)
        lo_w = sb("lo_w", [128, NW, KP], F16)
        iota_key = sb("iota_key", [128, MW], F16)
        iota_lo = sb("iota_lo", [128, 128, KP], F16)
        win_base = sb("win_base", [128, NW], F32)
        self_row = sb("self_row", [128, 255], F16)
        self_cols = sb("self_cols", [128, MW], F16)

        early = ExitStack()
        sb = allocator(early)
        x_in = sb("x_in", [P, 4, D], F32)
        xn = sb("xn", [P, 2, D], F32)
        stat1 = sb("stat1", [P, T, 6], F32)
        mv1 = sb("mv1", [P, T, 2], F32)
        std1 = sb("std1", [P, T], F32)
        rstd1 = sb("rstd1", [P, T], F32)
        W_raw = sb("W_raw", [128, KC, D], F32)
        dst_i = sb("dst_i", [P, CPP * CH], I32)
        src_i = sb("src_i", [P, CPP * CH], I32)
        edge_a = sb("edge_a", [P, CPP, CH], F32)
        edge_rows_sb = sb("edge_rows_sb", [P, CPP, 2, CH], F32)
        pad_rows = sb("pad_rows", [ROWS - NCH, 2 * CH], F32)
        spans = sb("spans", [P, 2, CPP], F32)
        spans_b = sb("spans_b", [NW, 2, NCH], F32)
        hit = sb("hit", [NW, 2, NCH], F32)
        chunk_up = sb("chunk_up", [NW, NCH], F32)
        chunk_down = sb("chunk_down", [NW, NCH], F32)
        win_lo = sb("win_lo", [NW, 1], F32)
        win_hi = sb("win_hi", [NW, 1], F32)
        first = sb("first", [NW, 2], F32)
        span_i = sb("span_i", [NW, 2], I32)
        flaw = sb("flaw", [P, 4], F32)
        slot_iota = sb("slot_iota", [NW, KS], F32)
        slot_i = sb("slot_i", [NW, KS], I32)
        early.close()

        late = ExitStack()
        sb = allocator(late)
        hT_hi = sb("hT_hi", [128, KC, GN], F32R)
        hT_lo = sb("hT_lo", [128, KC, GN], F32R)
        h1 = sb("h1", [128, 2, GN], F32)
        h1_hi = sb("h1_hi", [128, KC, GN], F32R)
        h1_lo = sb("h1_lo", [128, KC, GN], F32R)
        x_res = sb("x_res", [P, 2, D], F32)
        x2 = sb("x2", [P, 2, D], F32)
        xt = sb("xt", [P, 2, D], F32)
        stat2 = sb("stat2", [P, 2, 6], F32)
        mv2 = sb("mv2", [P, 2, 2], F32)
        std2 = sb("std2", [P, 2], F32)
        rstd2 = sb("rstd2", [P, 2], F32)
        late.close()
        graph.close()

        ffn = ExitStack()
        sb = allocator(ffn)
        Wg_raw = sb("Wg_raw", [128, KC, NE], F32)
        Wg_hi, Wg_lo = (sb(n, [128, KC, NE], F32R) for n in ("Wg_hi", "Wg_lo"))
        e_raw = sb("e_raw", [128, 2, 1024], F32)
        eW1_hi, eW1_lo = (sb(n, [128, NE, KC, H], F32R) for n in ("eW1_hi", "eW1_lo"))
        eW2_hi, eW2_lo = (sb(n, [128, NE, HC, D], F32R) for n in ("eW2_hi", "eW2_lo"))
        eb1_col = sb("eb1_col", [128, NE, HC], F32)
        eb2_sb = sb("eb2_sb", [NE, D], F32)
        xt_in = sb("xt_in", [P, 2, D], F32)
        xT_hi = sb("xT_hi", [128, KC, GN], F32R)
        xT_lo = sb("xT_lo", [128, KC, GN], F32R)
        gl = sb("gl", [P, 4, NE], F32)
        gm = sb("gm", [P, 4, 4], F32)
        top = sb("top", [P, 4, 8], F32)
        topi = sb("topi", [P, 4, 8], U32)
        topf = sb("topf", [P, 4, 2], F32)
        sc_a = sb("sc_a", [P, 4, NE], F32)
        score = sb("score", [P, 4, NE], F32)
        scoreT = sb("scoreT", [NE, 4, P], F32)
        he = sb("he", [128, HC, GN], F32)
        he_hi = sb("he_hi", [128, HC, GN], F32R)
        he_lo = sb("he_lo", [128, HC, GN], F32R)
        acc = sb("acc", [P, 4, D], F32)
        ffn.close()

        psum = ctx.enter_context(nc.psum_tensor("psum", [128, 8, 512], F32))
        WIN, AGG, SM = 0, 2, 6

        names = ("dst_in src_in x_in_a x_in_b x_in_c x_in_d w1_in w2_in small_in tables spans_out spans_in rows_out gathered "
                 "stats_ready std_ready xn_ready xn_hi_ready xn_lo_ready x_used "
                 "w_split w_raw_used idx_ready rows_turned rows_used hot_ready win_done counts_ready agg_done "
                 "hT_hi_ready hT_ready mlp1_done relu_ready h1_split mlp2_done x2_ready std2_ready xt_ready "
                 "res_in_a res_in_b res_sum x2_out_a x2_out_b dve_step act_step pool_step "
                 "ew_in_a ew_in_b ew_split xt_in_a xt_in_b turned xT_hi_ready xT_ready gated exp_ready score_ready scoreT_done scoreT_ready "
                 "next_blank next_in flaws_ready flaws_done range_ready range_out range_in gen_turned gen_taken gen_free gen_ready gen_win gen_split gen_stored gen_saved "
                 "gen_cleared gen_half counts_final counts_in agg_main rest_in "
                 "base_done base_added gate_done spans_ready keys_ready up_done gelu_ready he_split down_done summed x2_in out_done out_done_b").split()
        S = {n: sem(n) for n in names}

        block = ctx.enter_context(nc.Block())
        x_tiles = x.rearrange("(p t) d -> p t d", t=T)
        x_in_sems = [S["x_in_a"], S["x_in_b"], S["x_in_c"], S["x_in_d"]]
        res_in = [S["res_in_a"], S["res_in_b"]]
        x2_out = [S["x2_out_a"], S["x2_out_b"]]
        ew_in = [S["ew_in_a"], S["ew_in_b"]]
        xt_ins = [S["xt_in_a"], S["xt_in_b"]]

        def stepper(eng, s):
            count = [0]

            def step(ins):
                ins.then_inc(s, 1)
                count[0] += 1
                eng.wait_ge(s, count[0])
            return step

        def mlp1_chunks(part):
            return {0: (0, 1), 1: (2, 3)}.get(part, ())

        def mlp2_tiles(part):
            return {3: (0, 1), 4: (2, 3)}.get(part, ())

        @block.sync
        def _(sp):
            sp.dma_start(dst_i[:], dst.rearrange("(p e) -> p e", p=P)).then_inc(S["dst_in"], 16)
            sp.dma_start(src_i[:], src.rearrange("(p e) -> p e", p=P)).then_inc(S["src_in"], 16)
            sp.wait_ge(S["next_blank"], 1)
            row = CPP * CH
            for n, ahead in enumerate((1, FULL)):
                sp.dma_start(dst_next[0:P - 1, n], dst[ahead:ahead + (P - 1) * row].rearrange("(p e) -> p e", e=row))\
                  .then_inc(S["next_in"], 16)
                sp.dma_start(dst_next[P - 1:P, n, 0:row - ahead], dst[ahead + (P - 1) * row:E].rearrange("(o e) -> o e", o=1))\
                  .then_inc(S["next_in"], 16)
            for t in range(T):
                if t == 4:
                    sp.wait_ge(S["spans_ready"], 1)
                    sp.dma_start(spans_d.rearrange("a (p c) -> p a c", p=P), spans[:]).then_inc(S["spans_out"], 16)
                    sp.wait_ge(S["tables"], 1)
                    sp.dma_start(edge_rows[NCH:ROWS, :], pad_rows[:]).then_inc(S["rows_out"], 16)
                    sp.wait_ge(S["keys_ready"], 1)
                    sp.dma_start(edge_rows[0:NCH, :].rearrange("(p c) e -> p (c e)", p=P),
                                 edge_rows_sb[:].rearrange("p c a e -> p (c a e)")).then_inc(S["rows_out"], 16)
                    sp.wait_ge(S["spans_out"], 16)
                    sp.dma_start(spans_b[:], spans_d.rearrange("(o a) c -> o a c", o=1).broadcast_to([NW, 2, NCH])).then_inc(S["spans_in"], 16)
                if t >= 4:
                    sp.wait_ge(S["xn_ready"], t - 3)
                sp.dma_start(x_in[:, t % 4], x_tiles[:, t]).then_inc(x_in_sems[t % 4], 16)
            sp.wait_ge(S["range_ready"], 2)
            sp.dma_start(range_d[0, 0:2 * NW].rearrange("(w a) -> w a", a=2), span_i[:]).then_inc(S["range_out"], 16)
            sp.dma_start(range_d[:, 2 * NW:], flag_i[:]).then_inc(S["range_out"], 16)
            sp.wait_ge(S["range_out"], 32)
            sp.dma_start(range_row[:], range_d[:, :]).then_inc(S["range_in"], 16)
            sp.wait_ge(S["range_in"], 16)
            flag = sp.value_load(range_row[0:1, 2 * NW:], min_val=0, max_val=1)

            with sp.If(flag > 0):
                sp.sem_inc(S["gen_stored"], 1)
                with sp.Fori(0, NW) as w:
                    sp.wait_ge(S["gen_split"], w + 1)
                    for n in range(2):
                        sp.dma_start(counts_d[n, :, :, bass.ds(w * W, W)], gen_counts[:, n]).then_inc(S["gen_saved"], 16)
                    sp.wait_ge(S["gen_saved"], (w + 1) * 32)
                    sp.sem_inc(S["gen_stored"], 1)

            def store(g, tiles):
                for q in tiles:
                    n = 4 * g + q
                    rows = slice(n * P, (n + 1) * P)
                    sp.wait_ge(S["xt_ready"], n + 1)
                    sp.dma_start(x2_d[rows, :], x2[:, q % 2]).then_inc(x2_out[q % 2], 16)
                    sp.dma_start(xt_d[rows, :], xt[:, q % 2]).then_inc(x2_out[q % 2], 16)

            def group_counts(n, g):
                return counts[:, g % 2], counts_d[n, :, :, g * GN:(g + 1) * GN]

            for it in range(G + 3):
                if 0 <= it - 3:
                    store(it - 3, (2, 3))
                if 0 <= it - 2 < G:
                    store(it - 2, (0, 1))
                if 0 <= it - 1 < G:
                    with sp.If(flag > 0):
                        sp.wait_ge(S["agg_main"], it)
                        sp.dma_start(*group_counts(1, it - 1)).then_inc(S["rest_in"], 16)
                if it < G:
                    sp.wait_ge(S["counts_ready"], WG * (it + 1))
                    with sp.If(flag > 0):
                        sp.dma_start(*group_counts(0, it)).then_inc(S["counts_in"], 16)
                        sp.wait_ge(S["counts_in"], 16 * (it + 1))
                    sp.sem_inc(S["counts_final"], 1)
            for b in range(2):
                sp.wait_ge(x2_out[b], 32 * 2 * G)
            sp.dma_start(Wg_raw[:], Wg.rearrange("(k p) e -> p k e", p=128)).then_inc(S["small_in"], 16)
            for e in range(2 * NE):
                if e >= 2:
                    sp.wait_ge(S["ew_split"], e - 1)
                v = (eW1[e // 2].rearrange("(k p) h -> p k h", p=128) if e % 2 == 0
                     else eW2[e // 2].rearrange("(k p) h -> p k h", p=128))
                sp.dma_start(e_raw[:, e % 2].rearrange("p (k h) -> p k h", k=v.shape[1]), v).then_inc(ew_in[e % 2], 16)
            for n in range(T):
                g, q = divmod(n, 4)
                if n >= 2:
                    sp.wait_ge(S["turned"], n - 1)
                sp.dma_start(xt_in[:, n % 2], xt_d[n * P:(n + 1) * P, :]).then_inc(xt_ins[n % 2], 16)
                if q == 3:
                    if g >= 1:
                        sp.wait_ge(S["summed"], 4 * NE * g)
                        sp.dma_start(out.rearrange("(g q p) d -> g p q d", g=G, q=4)[g - 1], acc[:]).then_inc(S["out_done"], 16)
                        sp.wait_ge(S["out_done"], 16 * g)
                    sp.dma_start(acc[:], x2_d.rearrange("(g q p) d -> g p q d", g=G, q=4)[g]).then_inc(S["x2_in"], 16)
            sp.wait_ge(S["summed"], 4 * NE * G)
            sp.dma_start(out.rearrange("(g q p) d -> g p q d", g=G, q=4)[G - 1], acc[:]).then_inc(S["out_done"], 16)
            sp.wait_ge(S["out_done"], 16 * G)

        @block.gpsimd
        def _(pool):
            step = stepper(pool, S["pool_step"])
            small = dict(allow_small_or_imprecise_dtypes=True)
            pool.memset(dst_next[:, 0], N)
            pool.memset(dst_next[:, 1], -1).then_inc(S["next_blank"], 1)
            pool.memset(ones[:], 1.0)
            pool.iota(chunk_up[:], pattern=[[1, NCH]], base=1, channel_multiplier=0, **small)
            pool.iota(chunk_down[:], pattern=[[-1, NCH]], base=NCH, channel_multiplier=0, **small)
            pool.iota(win_lo[:], pattern=[[0, 1]], base=0, channel_multiplier=W, **small)
            pool.iota(win_hi[:], pattern=[[0, 1]], base=W - 1, channel_multiplier=W, **small)
            pool.iota(slot_iota[:], pattern=[[1, KS]], base=0, channel_multiplier=0, **small)
            pool.memset(pad_rows[:, 0:CH], FAR)
            pool.memset(pad_rows[:, CH:2 * CH], -1.0).then_inc(S["tables"], 1)
            pool.memset(ident[:], 0.0)
            pool.memset(eps_t[:], EPS)
            pool.iota(iota_e[:], pattern=[[1, NE]], base=0, channel_multiplier=0, **small)
            pool.memset(lo_w[:], -1.0)
            pool.memset(self_row[:], 0.0)
            step(pool.memset(self_cols[:], 0.0))
            pool.affine_select(out=ident[:], in_=ident[:], compare_op=ALU.not_equal, fill=1.0, base=0,
                               pattern=[[-1, 128]], channel_multiplier=1)
            pool.affine_select(out=self_row[:], in_=self_row[:], compare_op=ALU.not_equal, fill=1.0, base=127,
                               pattern=[[-1, 255]], channel_multiplier=1000)
            cols = self_cols[:].rearrange("p (w h) -> p w h", w=W)
            pool.affine_select(out=cols, in_=cols, compare_op=ALU.not_equal, fill=1.0, base=0,
                               pattern=[[1, W], [-1, T]], channel_multiplier=0)
            pool.iota(iota_key[:], pattern=[[1, MW]], base=0, channel_multiplier=0, **small)
            pool.iota(iota_lo[:], pattern=[[1, 128], [0, KP]], base=0, channel_multiplier=0, **small)
            pool.iota(win_base[:], pattern=[[MW, NW]], base=0, channel_multiplier=0, **small).then_inc(S["tables"], 1)

            def low_parts(a, b):
                for t in range(a, b):
                    pool.wait_ge(S["xn_hi_ready"], t + 1)
                    pool.tensor_tensor(xn_lo[:, t], xn[:, t % 2], xn_hi[:, t], ALU.subtract).then_inc(S["xn_lo_ready"], 1)

            low_parts(0, LOOK)
            pool.wait_ge(S["idx_ready"], 1)
            pool.wait_ge(S["rows_out"], 32)
            for k in range(KS):
                pool.indirect_dma_start(out=slot_rows[:, k], out_offset=None, in_=edge_rows[:, :],
                                        in_offset=bass.IndirectOffsetOnAxis(ap=slot_i[:, k:k + 1], axis=0),
                                        bounds_check=ROWS - 1).then_inc(S["gathered"], 16)
            low_parts(LOOK, T)
            for n, (hi, lo, s) in enumerate(((W1_hi, W1_lo, S["w1_in"]), (W2_hi, W2_lo, S["w2_in"]))):
                pool.wait_ge(s, 16)
                step(pool.tensor_copy(hi[:], W_raw[:]))
                pool.tensor_tensor(lo[:], W_raw[:], hi[:].bitcast(F32), ALU.subtract).then_inc(S["w_split"], 1)

            for g in range(G):
                for m in range(KC):
                    pool.wait_ge(S["relu_ready"], 4 * g + m + 1)
                    if m == 0 and g >= 1:
                        pool.wait_ge(S["mlp2_done"], 4 * g)
                    step(pool.tensor_copy(h1_hi[:, m], h1[:, m % 2]))
                    pool.tensor_tensor(h1_lo[:, m], h1[:, m % 2], h1_hi[:, m].bitcast(F32), ALU.subtract)\
                        .then_inc(S["h1_split"], 1)
                for q in range(4):
                    pool.wait_ge(res_in[q % 2], 16 * (2 * g + q // 2 + 1))
                    pool.tensor_tensor(x_res[:, q % 2], x_res[:, q % 2], b2_row[:], ALU.add).then_inc(S["res_sum"], 1)

            for e in range(2 * NE):
                hi, lo = ((eW1_hi, eW1_lo) if e % 2 == 0 else (eW2_hi, eW2_lo))
                pool.wait_ge(ew_in[e % 2], 16 * (e // 2 + 1))
                hv, lv = (v[:, e // 2].rearrange("p k h -> p (k h)") for v in (hi, lo))
                step(pool.tensor_copy(hv, e_raw[:, e % 2]))
                pool.tensor_tensor(lv, e_raw[:, e % 2], hv.bitcast(F32), ALU.subtract).then_inc(S["ew_split"], 1)

        @block.scalar
        def _(act):
            step = stepper(act, S["act_step"])
            for n, (raw, s) in enumerate(((gW1, S["w1_in"]), (gW2, S["w2_in"]))):
                if n:
                    act.wait_ge(S["w_split"], 1)
                act.dma_start(W_raw[:], raw.rearrange("(k p) n -> p k n", p=128)).then_inc(s, 16)
                if n == 0:
                    act.dma_start(b1_col[:], gb1.rearrange("(k p) -> p k", p=128), allow_slow_non_contiguous=True).then_inc(S["small_in"], 16)
                    act.dma_start(b2_row[:], gb2.rearrange("(o n) -> o n", o=1).broadcast_to([P, D])).then_inc(S["small_in"], 16)
                    act.wait_ge(S["tables"], 2)
                    for t in range(T):
                        act.wait_ge(S["stats_ready"], t + 1)
                        act.activation(std1[:, t:t + 1], mv1[:, t, 1:2], ACT.Sqrt, bias=eps_t[0:P, 0:1]).then_inc(S["std_ready"], 1)
                        if t >= 1:
                            act.wait_ge(S["xn_ready"], t)
                            act.activation(xn_hi[:, t - 1], xn[:, (t - 1) % 2], ACT.Copy).then_inc(S["xn_hi_ready"], 1)
                    act.wait_ge(S["xn_ready"], T)
                    act.activation(xn_hi[:, T - 1], xn[:, (T - 1) % 2], ACT.Copy).then_inc(S["xn_hi_ready"], 1)

            def load_residual(g, q):
                n = 4 * g + q
                if n >= 2:
                    act.wait_ge(S["x2_ready"], n - 1)
                act.dma_start(x_res[:, q % 2], x[n * P:(n + 1) * P, :]).then_inc(res_in[q % 2], 16)

            def std2s(g, tiles):
                for q in tiles:
                    act.wait_ge(S["x2_ready"], 4 * g + q + 1)
                    act.activation(std2[:, q % 2:q % 2 + 1], mv2[:, q % 2, 1:2], ACT.Sqrt, bias=eps_t[0:P, 0:1])\
                       .then_inc(S["std2_ready"], 1)
                    if q < 2:
                        load_residual(g, q + 2)

            for it in range(G + 3):
                g = it - 2
                for part in range(PARTS):
                    if 0 <= g < G and part == 0:
                        if g == 0:
                            act.wait_ge(S["w_split"], 2)
                        act.wait_ge(S["agg_done"], g + 1)
                        for c in range(KC):
                            if c == 0 and g >= 1:
                                act.wait_ge(S["mlp1_done"], 4 * g)
                            act.activation(hT_hi[:, c], psum[:, AGG + c, 0:GN], ACT.Copy).then_inc(S["hT_hi_ready"], 1)
                    if part == 0 and 0 <= g - 1 < G:
                        std2s(g - 1, (2, 3))
                    if part == 4 and 0 <= g < G:
                        std2s(g, (0, 1))
                    for j in range(WP):
                        if it < G:
                            w = WG * it + WP * part + j
                            act.wait_ge(S["win_done"], w + 1)
                            if part == 0 and j == 0 and it >= 2:
                                act.wait_ge(S["agg_done"], it - 1)
                            place = W * (WP * part + j)
                            act.activation(counts[:, it % 2, :, place:place + W],
                                           psum[:, WIN + j % 2, 0:MW].rearrange("p (w h) -> p h w", w=W),
                                           ACT.Copy).then_inc(S["counts_ready"], 1)
                    if 0 <= g < G:
                        for m in mlp1_chunks(part):
                            act.wait_ge(S["mlp1_done"], 4 * g + m + 1)
                            if 4 * g + m >= 2:
                                act.wait_ge(S["h1_split"], 4 * g + m - 1)
                            act.activation(h1[:, m % 2], psum[:, SM + m % 2, 0:GN], ACT.Relu, bias=b1_col[:, m:m + 1])\
                               .then_inc(S["relu_ready"], 1)
                        if part == 2:
                            load_residual(g, 0)
                            load_residual(g, 1)

            for g in range(G):
                for q in range(4):
                    n = 4 * g + q
                    act.wait_ge(S["turned"], n + 1)
                    if q == 0 and g >= 1:
                        act.wait_ge(S["up_done"], HC * NE * g)
                    act.activation(xT_hi[:, :, q * P:(q + 1) * P], psum[:, n % 2, 0:4 * P].rearrange("p (c n) -> p c n", c=KC), ACT.Copy)\
                       .then_inc(S["xT_hi_ready"], 1)
                act.wait_ge(S["gated"], g + 1)
                for q in range(4):
                    ins = act.activation(gl[:, q], gl[:, q], ACT.Exp, bias=gm[:, q, 0:1], accum_out=gm[:, q, 1:2])
                ins.then_inc(S["exp_ready"], 1)
                if g == 0:
                    act.dma_start(eb1_col[:], eb1.rearrange("e (k p) -> p e k", p=128), allow_slow_non_contiguous=True).then_inc(S["small_in"], 16)
                    act.dma_start(eb2_sb[:], eb2[:, :]).then_inc(S["small_in"], 16)
                    act.wait_ge(S["small_in"], 80)
                act.wait_ge(S["scoreT_done"], g + 1)
                act.activation(scoreT[:], psum[0:NE, 2, 0:4 * P].rearrange("p (q n) -> p q n", q=4), ACT.Copy)\
                   .then_inc(S["scoreT_ready"], 1)
                for e in range(NE):
                    for m in range(HC):
                        n = (g * NE + e) * HC + m
                        act.wait_ge(S["up_done"], n + 1)
                        if n >= HC:
                            act.wait_ge(S["he_split"], n - 1)
                        act.activation(he[:, m], psum[:, 3 + m, 0:GN], ACT.Gelu, bias=eb1_col[:, e, m:m + 1])\
                           .then_inc(S["gelu_ready"], 1)

        @block.vector
        def _(dve):
            step = stepper(dve, S["dve_step"])
            key_part, lo_part = edge_rows_sb[:, :, 0], edge_rows_sb[:, :, 1]
            dve.wait_ge(S["dst_in"], 16)
            dst_v = dst_i[:].rearrange("p (c e) -> p c e", c=CPP)
            src_v = src_i[:].rearrange("p (c e) -> p c e", c=CPP)
            dve.tensor_reduce(spans[:, 0], dst_v, AX.X, ALU.min)
            dve.tensor_reduce(spans[:, 1], dst_v, AX.X, ALU.max).then_inc(S["spans_ready"], 1)
            dve.wait_ge(S["src_in"], 16)
            step(dve.tensor_scalar(lo_part, src_v, 1.0 / T, 0.5 / T - 0.5, ALU.mult, ALU.add))
            step(dve.tensor_scalar(lo_part, lo_part, ROUND, ROUND, ALU.add, ALU.subtract))
            step(dve.scalar_tensor_tensor(edge_a[:], lo_part, -float(T), src_v, ALU.mult, ALU.add))
            dve.scalar_tensor_tensor(key_part, dst_v, float(T), edge_a[:], ALU.mult, ALU.add).then_inc(S["keys_ready"], 1)

            def normalise(t):
                dve.wait_ge(x_in_sems[t % 4], 16 * (t // 4 + 1))
                step(dve.bn_stats(stat1[:, t], x_in[:, t % 4]))
                dve.bn_aggr(mv1[:, t], stat1[:, t]).then_inc(S["stats_ready"], 1)

            def normalise_end(t):
                dve.wait_ge(S["std_ready"], t + 1)
                step(dve.reciprocal(rstd1[:, t:t + 1], std1[:, t:t + 1]))
                if t >= 2:
                    dve.wait_ge(S["xn_lo_ready"], t - 1)
                ins = dve.tensor_scalar(xn[:, t % 2], x_in[:, t % 4], mv1[:, t, 0:1], rstd1[:, t:t + 1],
                                        ALU.subtract, ALU.mult)
                ins.then_inc(S["xn_ready"], 1)

            def find_windows():
                dve.wait_ge(S["tables"], 1)
                dve.wait_ge(S["spans_in"], 16)
                step(dve.tensor_scalar(hit[:, 0], spans_b[:, 0], win_hi[:], None, ALU.is_le))
                step(dve.scalar_tensor_tensor(hit[:, 0], spans_b[:, 1], win_lo[:], hit[:, 0], ALU.is_ge, ALU.mult))
                step(dve.tensor_tensor(hit[:, 1], hit[:, 0], chunk_down[:], ALU.mult))
                step(dve.tensor_reduce(first[:, 0:1], hit[:, 1], AX.X, ALU.max))
                step(dve.tensor_scalar(first[:, 1:2], first[:, 0:1], -1.0, float(NCH), ALU.mult, ALU.add))
                dve.tensor_scalar(slot_i[:], slot_iota[:], first[:, 1:2], None, ALU.add).then_inc(S["idx_ready"], 1)
                step(dve.tensor_tensor(hit[:, 1], hit[:, 0], chunk_up[:], ALU.mult))
                step(dve.tensor_reduce(first[:, 0:1], hit[:, 1], AX.X, ALU.max))
                step(dve.tensor_copy(span_i[:, 0:1], first[:, 1:2]))
                step(dve.scalar_tensor_tensor(span_i[:, 1:2], first[:, 1:2], 1.0, first[:, 0:1], ALU.add, ALU.max))
                step(dve.scalar_tensor_tensor(flaw[:, 0:1], first[:, 1:2], float(KS), first[:, 0:1], ALU.add, ALU.is_lt))
                dve.wait_ge(S["next_in"], 64)
                for n, op in enumerate((ALU.is_gt, ALU.is_equal)):
                    step(dve.tensor_tensor(edge_a[:].rearrange("p c e -> p (c e)"), dst_i[:], dst_next[:, n], op))
                    step(dve.tensor_reduce(flaw[:, n + 1:n + 2], edge_a[:], AX.XY, ALU.max))
                step(dve.tensor_reduce(flaw[:, 3:4], flaw[:, 0:3], AX.X, ALU.add))
                dve.tensor_copy(flaw[:, 0:1], flaw[:, 3:4]).then_inc(S["flaws_ready"], 1)

            def take_rows(k):
                at = 256 * (k % 2)
                dve.tensor_tensor(key_w[:, k], psum[:, AGG + k // 2, at:at + NW], win_base[:], ALU.subtract)
                dve.tensor_copy(lo_w[:, :, k], psum[:, AGG + k // 2, at + 128:at + 128 + NW]).then_inc(S["rows_used"], 1)

            for t in range(T):
                normalise(t)
                if t >= 1:
                    normalise_end(t - 1)
                if t == LOOK:
                    find_windows()
            normalise_end(T - 1)
            dve.wait_ge(S["tables"], 2)
            dve.wait_ge(S["rows_turned"], KS)
            for k in range(KS):
                take_rows(k)
            dve.wait_ge(S["rows_used"], KS)
            dve.wait_ge(S["flaws_done"], 1)
            dve.tensor_scalar(flag_i[:], psum[0:1, SM, 0:1], 1.0, None, ALU.min).then_inc(S["range_ready"], 2)

            dve.wait_ge(S["range_in"], 16)
            flag = dve.value_load(range_row[0:1, 2 * NW:], min_val=0, max_val=1)
            with dve.If(flag > 0):
                dve.memset(key_all[:], FAR)
                dve.memset(lo_all[:], -1.0).then_inc(S["gen_cleared"], 1)
                dve.wait_ge(S["gen_cleared"], 1)
                dve.wait_ge(S["gen_turned"], 1)
                for n, (table, j) in enumerate((table, j) for table in (key_all, lo_all) for j in range(CPP)):
                    place = table[:, 0:NCH].rearrange("p (c j) -> p j c", j=CPP)[:, j]
                    dve.tensor_copy(place, psum[:, AGG + n // 4, 128 * (n % 4):128 * (n % 4) + P]).then_inc(S["gen_taken"], 1)
                dve.wait_ge(S["gen_taken"], 2 * CPP)
                visit = dve.alloc_register("dve_visit")
                dve.reg_mov(visit, 0)
                with dve.Fori(0, NW) as w:
                    start = dve.value_load(range_row[0:1, bass.ds(w * 2, 1)], min_val=0, max_val=NCH)
                    end = dve.value_load(range_row[0:1, bass.ds(w * 2 + 1, 1)], min_val=1, max_val=NCH + 1)
                    with dve.Fori(start, end) as c:
                        n = dve.snap(visit, min_val=0, max_val=NW * NCH)
                        dve.wait_ge(S["gen_free"], n + 1)
                        dve.tensor_scalar(gen_key[:], iota_key[:], win_base[:, bass.ds(w, 1)], key_all[:, bass.ds(c, 1)],
                                          ALU.add, ALU.is_equal)
                        dve.tensor_scalar(gen_lo[:], iota_lo[:, :, 0], lo_all[:, bass.ds(c, 1)], None, ALU.is_equal)\
                           .then_inc(S["gen_ready"], 1)
                        dve.reg_add(visit, visit, 1)
                    dve.wait_ge(S["gen_win"], w + 1)
                    dve.wait_ge(S["gen_stored"], w + 1)
                    total = psum[:, WIN, 0:MW].rearrange("p (w h) -> p h w", w=W)
                    dve.tensor_copy(gen_counts[:, 0], total).then_inc(S["gen_half"], 1)
                    dve.wait_ge(S["gen_half"], w + 1)
                    dve.tensor_tensor(gen_counts[:, 1], total, gen_counts[:, 0], ALU.subtract).then_inc(S["gen_split"], 1)
                dve.wait_ge(S["gen_stored"], NW + 1)

            def one_hots(w):
                if w >= RING:
                    dve.wait_ge(S["win_done"], w - RING + 1)
                for k in range(KS):
                    dve.tensor_scalar(hot_key[:, w % RING, k], iota_key[:], key_w[:, k, w:w + 1], None, ALU.is_equal)
                dve.tensor_tensor(hot_lo[:, w % RING], iota_lo[:],
                                  lo_w[:, w].rearrange("p (o k) -> p o k", o=1).broadcast_to([128, 128, KP]),
                                  ALU.is_equal).then_inc(S["hot_ready"], 1)

            def split_sums(g):
                if g == 0:
                    dve.wait_ge(S["w_split"], 2)
                for c in range(KC):
                    dve.wait_ge(S["hT_hi_ready"], 4 * g + c + 1)
                    dve.tensor_tensor(hT_lo[:, c], psum[:, AGG + c, 0:GN], hT_hi[:, c].bitcast(F32), ALU.subtract)\
                       .then_inc(S["hT_ready"], 1)

            def residual(g, q):
                n = 4 * g + q
                dve.wait_ge(S["mlp2_done"], n + 1)
                dve.wait_ge(S["res_sum"], n + 1)
                if n >= 2:
                    dve.wait_ge(x2_out[q % 2], 32 * (2 * g + q // 2))
                step(dve.tensor_tensor(x2[:, q % 2], psum[0:P, SM + q % 2, :], x_res[:, q % 2], ALU.add))
                step(dve.bn_stats(stat2[:, q % 2], x2[:, q % 2]))
                dve.bn_aggr(mv2[:, q % 2], stat2[:, q % 2]).then_inc(S["x2_ready"], 1)

            def residual_end(g, q):
                n = 4 * g + q
                dve.wait_ge(S["std2_ready"], n + 1)
                step(dve.reciprocal(rstd2[:, q % 2:q % 2 + 1], std2[:, q % 2:q % 2 + 1]))
                dve.tensor_scalar(xt[:, q % 2], x2[:, q % 2], mv2[:, q % 2, 0:1], rstd2[:, q % 2:q % 2 + 1],
                                  ALU.subtract, ALU.mult).then_inc(S["xt_ready"], 1)

            for it in range(G + 3):
                g = it - 2
                for part in range(PARTS):
                    for j in range(WP):
                        if it < G:
                            one_hots(WG * it + WP * part + j)
                        if j == RING - 1:
                            if part == 0:
                                if 0 <= g < G:
                                    split_sums(g)
                                if 0 <= g - 1 < G:
                                    for q in (2, 3):
                                        residual(g - 1, q)
                                    for q in (2, 3):
                                        residual_end(g - 1, q)
                            elif 0 <= g < G and part == 4:
                                for q in (0, 1):
                                    residual(g, q)
                                for q in (0, 1):
                                    residual_end(g, q)

            for g in range(G):
                for q in range(4):
                    n = 4 * g + q
                    dve.wait_ge(S["xT_hi_ready"], n + 1)
                    dve.tensor_tensor(xT_lo[:, :, q * P:(q + 1) * P], psum[:, n % 2, 0:4 * P].rearrange("p (c n) -> p c n", c=KC),
                                      xT_hi[:, :, q * P:(q + 1) * P].bitcast(F32), ALU.subtract).then_inc(S["xT_ready"], 1)
                if g == 0:
                    dve.wait_ge(S["small_in"], 48)
                    step(dve.tensor_copy(Wg_hi[:], Wg_raw[:]))
                    dve.tensor_tensor(Wg_lo[:], Wg_raw[:], Wg_hi[:].bitcast(F32), ALU.subtract).then_inc(S["w_split"], 1)
                dve.wait_ge(S["gate_done"], g + 1)
                lg = psum[0:P, 2, 0:4 * NE].rearrange("p (q e) -> p q e", q=4)
                step(dve.tensor_reduce(gm[:, :, 0:1], lg, AX.X, ALU.max))
                step(dve.tensor_scalar(gm[:, :, 0:1], gm[:, :, 0:1], -1.0, None, ALU.mult))
                dve.tensor_copy(gl[:], lg).then_inc(S["gated"], 1)
                dve.wait_ge(S["exp_ready"], g + 1)
                step(dve.reciprocal(gm[:, :, 2:3], gm[:, :, 1:2]))
                for q in range(4):
                    ins = dve.tensor_scalar(gl[:, q], gl[:, q], gm[:, q, 2:3], None, ALU.mult)
                step(ins)
                for q in range(4):
                    ins = dve.max(top[:, q], gl[:, q])
                step(ins)
                for q in range(4):
                    ins = dve.max_index(topi[:, q], top[:, q], gl[:, q])
                step(ins)
                step(dve.tensor_copy(topf[:], topi[:, :, 0:2]))
                step(dve.tensor_tensor(gm[:, :, 3:4], top[:, :, 0:1], top[:, :, 1:2], ALU.add))
                step(dve.tensor_scalar(gm[:, :, 3:4], gm[:, :, 3:4], 1e-6, None, ALU.add))
                step(dve.reciprocal(gm[:, :, 3:4], gm[:, :, 3:4]))
                for r in range(2):
                    for q in range(4):
                        ins = dve.tensor_scalar((score, sc_a)[r][:, q], iota_e[:], topf[:, q, r:r + 1], top[:, q, r:r + 1],
                                                ALU.is_equal, ALU.mult)
                step(ins)
                step(dve.tensor_tensor(score[:], score[:], sc_a[:], ALU.add))
                for q in range(4):
                    ins = dve.tensor_scalar(score[:, q], score[:, q], gm[:, q, 3:4], None, ALU.mult)
                ins.then_inc(S["score_ready"], 1)
                dve.wait_ge(S["x2_in"], 16 * (g + 1))
                for q in range(4):
                    dve.wait_ge(S["base_done"], 4 * g + q + 1)
                    dve.tensor_tensor(acc[:, q], psum[0:P, 5 + q % 2, :], acc[:, q], ALU.add).then_inc(S["base_added"], 1)
                dve.wait_ge(S["base_added"], 4 * (g + 1))
                for e in range(NE):
                    for m in range(HC):
                        n = (g * NE + e) * HC + m
                        dve.wait_ge(S["gelu_ready"], n + 1)
                        if n >= HC:
                            dve.wait_ge(S["down_done"], 4 * (g * NE + e))
                        step(dve.tensor_copy(he_hi[:, m], he[:, m]))
                        dve.tensor_tensor(he_lo[:, m], he[:, m], he_hi[:, m].bitcast(F32), ALU.subtract).then_inc(S["he_split"], 1)
                    for q in range(4):
                        n = 4 * (g * NE + e) + q
                        dve.wait_ge(S["down_done"], n + 1)
                        if e:
                            dve.wait_ge(S["summed"], n - 3)
                        dve.scalar_tensor_tensor(acc[:, q], psum[0:P, 5 + q % 2, :], score[:, q, e:e + 1], acc[:, q],
                                                 ALU.mult, ALU.add).then_inc(S["summed"], 1)

        @block.tensor
        def _(pe):
            mm = pe.matmul
            pe.wait_ge(S["tables"], 2)
            pe.wait_ge(S["gathered"], 16 * KS)
            for k in range(KS):
                at = 256 * (k % 2)
                pe.transpose(psum[:, AGG + k // 2, at:at + NW], slot_rows[:, k, 0:CH], ident[0:NW, 0:NW])
                pe.transpose(psum[:, AGG + k // 2, at + 128:at + 128 + NW], slot_rows[:, k, CH:2 * CH], ident[0:NW, 0:NW])\
                  .then_inc(S["rows_turned"], 1)

            pe.wait_ge(S["flaws_ready"], 1)
            mm(psum[0:1, SM, 0:1], flaw[:, 0:1], ones[:], start=True, stop=True).then_inc(S["flaws_done"], 1)
            pe.wait_ge(S["range_in"], 16)
            flag = pe.value_load(range_row[0:1, 2 * NW:], min_val=0, max_val=1)
            with pe.If(flag > 0):
                pe.wait_ge(S["rows_used"], KS)
                for n, (v, j) in enumerate((v, j) for v in range(2) for j in range(CPP)):
                    ins = pe.transpose(psum[:, AGG + n // 4, 128 * (n % 4):128 * (n % 4) + P], edge_rows_sb[:, j, v], ident[0:P, 0:P])
                ins.then_inc(S["gen_turned"], 1)
                pe.sem_inc(S["gen_free"], 1)
                visit = pe.alloc_register("pe_visit")
                pe.reg_mov(visit, 0)
                bank = psum[:, WIN, 0:MW]
                with pe.Fori(0, NW) as w:
                    start = pe.value_load(range_row[0:1, bass.ds(w * 2, 1)], min_val=0, max_val=NCH)
                    end = pe.value_load(range_row[0:1, bass.ds(w * 2 + 1, 1)], min_val=1, max_val=NCH + 1)
                    pe.wait_ge(S["gen_stored"], w + 1)
                    mm(bank, self_row[:, bass.ds(w * -1 + 127, 128)], self_cols[:], start=True, stop=False)
                    with pe.Fori(start, end) as c:
                        n = pe.snap(visit, min_val=0, max_val=NW * NCH)
                        pe.wait_ge(S["gen_ready"], n + 1)
                        mm(bank, gen_lo[:], gen_key[:], start=False, stop=False).then_inc(S["gen_free"], 1)
                        pe.reg_add(visit, visit, 1)
                    mm(psum[0:127, WIN, 0:MW], self_row[:, 128:255], self_cols[:], start=False, stop=True)\
                      .then_inc(S["gen_win"], 1)

            def window(w, j):
                free = {0: w, 1: w - 1}.get(j, w - 1)
                if free > 0:
                    pe.wait_ge(S["counts_ready"], free)
                pe.wait_ge(S["hot_ready"], w + 1)
                bank = psum[:, WIN + j % 2, 0:MW]
                mm(bank, self_row[:, 127 - w:255 - w], self_cols[:], start=True, stop=False)
                for k in range(KS):
                    ins = mm(bank, hot_lo[:, w % RING, :, k], hot_key[:, w % RING, k], start=False, stop=(k == KS - 1))
                ins.then_inc(S["win_done"], 1)

            def sums(g, part):
                if part == 0:
                    pe.wait_ge(S["counts_final"], g + 1)
                    if g >= 1:
                        pe.wait_ge(S["hT_ready"], 4 * g)
                for t in range(TP * part, TP * part + TP):
                    if g == 0:
                        pe.wait_ge(S["xn_hi_ready"], t + 1)
                        pe.wait_ge(S["xn_lo_ready"], t + 1)
                    for n, half in enumerate((xn_hi, xn_lo)):
                        for c in range(KC):
                            ins = mm(psum[:, AGG + c, 0:GN], half[:, t, c * 128:(c + 1) * 128], counts[0:P, g % 2, t],
                                     start=(t == 0 and n == 0), stop=(t == T - 1 and n == 1))
                if part == PARTS - 1:
                    ins.then_inc(S["agg_main"], 1)
                    with pe.If(flag > 0):
                        pe.wait_ge(S["rest_in"], 16 * (g + 1))
                        for t in range(T):
                            for half in (xn_hi, xn_lo):
                                for c in range(KC):
                                    mm(psum[:, AGG + c, 0:GN], half[:, t, c * 128:(c + 1) * 128], counts[0:P, g % 2, t],
                                       start=False, stop=(t == T - 1 and half is xn_lo), skip_group_check=True)
                    mm(psum[0:127, AGG + KC - 1, 0:MW], self_row[:, 128:255], self_cols[:], start=False, stop=True,
                       skip_group_check=True).then_inc(S["agg_done"], 1)

            def mlp1(g, m):
                if m == 0:
                    pe.wait_ge(S["hT_ready"], 4 * (g + 1))
                    pe.wait_ge(S["w_split"], 1)
                if m >= 2:
                    pe.wait_ge(S["relu_ready"], 4 * g + m - 1)
                elif g >= 1:
                    pe.wait_ge(S["x2_ready"], 4 * g + m - 1)
                cols = slice(m * 128, (m + 1) * 128)
                trio = [(W1_hi, hT_hi), (W1_lo, hT_hi), (W1_hi, hT_lo)]
                for k in range(KC):
                    for n, (w_, h_) in enumerate(trio):
                        ins = mm(psum[:, SM + m % 2, 0:GN], w_[:, k, cols], h_[:, k], start=(k == 0 and n == 0),
                                 stop=(k == KC - 1 and n == 2))
                ins.then_inc(S["mlp1_done"], 1)

            def mlp2(g, q):
                if q == 0:
                    pe.wait_ge(S["h1_split"], 4 * (g + 1))
                    pe.wait_ge(S["w_split"], 2)
                if q >= 2:
                    pe.wait_ge(S["x2_ready"], 4 * g + q - 1)
                rows = slice(q * P, (q + 1) * P)
                trio = [(h1_hi, W2_hi), (h1_hi, W2_lo), (h1_lo, W2_hi)]
                for k in range(KC):
                    for n, (h_, w_) in enumerate(trio):
                        ins = mm(psum[0:P, SM + q % 2, :], h_[:, k, rows], w_[:, k], start=(k == 0 and n == 0),
                                 stop=(k == KC - 1 and n == 2))
                ins.then_inc(S["mlp2_done"], 1)

            for it in range(G + 2):
                for part in range(PARTS):
                    if it < G:
                        for j in range(WP):
                            window(WG * it + WP * part + j, j)
                    if 0 <= it - 1 < G:
                        sums(it - 1, part)
                    if 0 <= it - 2:
                        for m in mlp1_chunks(part):
                            mlp1(it - 2, m)
                        for q in mlp2_tiles(part):
                            mlp2(it - 2, q)

            pe.wait_ge(S["x2_ready"], 4 * G)
            for g in range(G):
                for q in range(4):
                    n = 4 * g + q
                    pe.wait_ge(xt_ins[n % 2], 16 * (n // 2 + 1))
                    if n >= 2:
                        pe.wait_ge(S["xT_ready"], n - 1)
                    for c in range(KC):
                        ins = pe.transpose(psum[:, n % 2, c * P:(c + 1) * P], xt_in[:, n % 2, c * 128:(c + 1) * 128], ident[0:P, 0:P])
                    ins.then_inc(S["turned"], 1)
                pe.wait_ge(S["xT_ready"], 4 * (g + 1))
                if g == 0:
                    pe.wait_ge(S["w_split"], 3)
                if g >= 1:
                    pe.wait_ge(S["scoreT_ready"], g)
                for q in range(4):
                    rows = slice(q * P, (q + 1) * P)
                    quartet = [(a, b) for a in (xT_hi, xT_lo) for b in (Wg_hi, Wg_lo)]
                    for k in range(KC):
                        for n, (a, b) in enumerate(quartet):
                            ins = mm(psum[0:P, 2, q * NE:(q + 1) * NE], a[:, k, rows], b[:, k], start=(k == 0 and n == 0),
                                     stop=(k == KC - 1 and n == 3))
                ins.then_inc(S["gate_done"], 1)
                pe.wait_ge(S["score_ready"], g + 1)
                for q in range(4):
                    ins = pe.transpose(psum[0:NE, 2, q * P:(q + 1) * P], score[:, q], ident[0:P, 0:P])
                ins.then_inc(S["scoreT_done"], 1)
                pe.wait_ge(S["scoreT_ready"], g + 1)
                for q in range(4):
                    n = 4 * g + q
                    if q >= 2:
                        pe.wait_ge(S["base_added"], n - 1)
                    elif g >= 1:
                        pe.wait_ge(S["summed"], 4 * NE * g)
                    mm(psum[0:P, 5 + q % 2, :], scoreT[:, q], eb2_sb[:], start=True, stop=True).then_inc(S["base_done"], 1)
                for e in range(NE):
                    pe.wait_ge(S["ew_split"], 2 * NE if g else 2 * e + 2)
                    for m in range(HC):
                        n = (g * NE + e) * HC + m
                        if n >= HC:
                            pe.wait_ge(S["gelu_ready"], n - 1)
                        cols = slice(m * 128, (m + 1) * 128)
                        trio = [(eW1_hi, xT_hi), (eW1_lo, xT_hi), (eW1_hi, xT_lo)]
                        for k in range(KC):
                            for i, (w_, x_) in enumerate(trio):
                                ins = mm(psum[:, 3 + m, 0:GN], w_[:, e, k, cols], x_[:, k], start=(k == 0 and i == 0),
                                         stop=(k == KC - 1 and i == 2))
                        ins.then_inc(S["up_done"], 1)
                    pe.wait_ge(S["he_split"], HC * (g * NE + e + 1))
                    for q in range(4):
                        n = 4 * (g * NE + e) + q
                        if e == 0 and q < 2:
                            pe.wait_ge(S["base_added"], 4 * (g + 1))
                        else:
                            pe.wait_ge(S["summed"], n - 1)
                        rows = slice(q * P, (q + 1) * P)
                        trio = [(he_hi, eW2_hi), (he_hi, eW2_lo), (he_lo, eW2_hi)]
                        for k in range(HC):
                            for i, (h_, w_) in enumerate(trio):
                                ins = mm(psum[0:P, 5 + q % 2, :], h_[:, k, rows], w_[:, e, k], start=(k == 0 and i == 0),
                                         stop=(k == HC - 1 and i == 2))
                        ins.then_inc(S["down_done"], 1)


_INS = ["x", "src", "dst", "L0_gnn_W1", "L0_gnn_b1", "L0_gnn_W2", "L0_gnn_b2",
        "L0_ffn_Wg", "L0_ffn_W1", "L0_ffn_b1", "L0_ffn_W2", "L0_ffn_b2"]


def kernel(**inputs):
    import numpy as _np
    import concourse.bacc as _bacc
    from concourse.bass_utils import run_bass_kernel_spmd as _run

    nc = _bacc.Bacc("TRN2", target_bir_lowering=False, num_devices=1)
    arrays, args = {}, []
    for name in _INS:
        a = _np.ascontiguousarray(inputs[name])
        arrays[f"in_{name}"] = a
        args.append(nc.dram_tensor(f"in_{name}", a.shape, mybir.dt.from_np(a.dtype), kind="ExternalInput").ap())
    args.append(nc.dram_tensor("out_x", (N, D), F32, kind="ExternalOutput").ap())
    gnn_moe(nc, *args)
    r = _run(nc, [arrays], core_ids=[0])
    return r.results[0]["out_x"]
```

```python
from contextlib import ExitStack

import concourse.bass as bass
from concourse import mybir

F32 = mybir.dt.float32
F32R = mybir.dt.float32r
F16 = mybir.dt.float16
BF16 = mybir.dt.bfloat16
I32 = mybir.dt.int32
U32 = mybir.dt.uint32
ALU = mybir.AluOpType
ACT = mybir.ActivationFunctionType
AX = mybir.AxisListType

N, D, E = 2500, 512, 80000
P = 125
T = N // P
KC = D // 128
CH = 128
NCH = E // CH
CPP = NCH // P
W = 20
NW = N // W
MW = W * T
KS = 7
FULL = 255
KP = 8
ROWS = 640
G = 5
GN = N // G
WG = NW // G
PARTS = 5
WP = WG // PARTS
TP = T // PARTS
LOOK = 6
RING = 4
NE, H, HC = 8, 256, 2
B = 256
NB = (2 * N + NE * (B - 1)) // B
NT = 2 * (NB + 1)
FAR = -1.0e6
EPS = 1e-5
ROUND = 12582912.0


def gnn_moe(nc, x, src, dst, gW1, gb1, gW2, gb2, Wg, eW1, eb1, eW2, eb2, out):
    ctx = ExitStack()
    with ctx:
        def sem(name):
            return ctx.enter_context(nc.semaphore(name))

        def allocator(stack):
            return lambda name, shape, dt: stack.enter_context(nc.sbuf_tensor(name, shape, dt))

        edge_rows = nc.dram_tensor("edge_rows", [ROWS, 2 * CH], F32).ap()
        spans_d = nc.dram_tensor("spans_d", [2, NCH], F32).ap()
        x2_d = nc.dram_tensor("x2_d", [N, D], F32).ap()
        xt_d = nc.dram_tensor("xt_d", [N, D], F32).ap()
        y_d = nc.dram_tensor("y_d", [NB * B, D], F32).ap()
        range_d = nc.dram_tensor("range_d", [1, 2 * NW + 1], I32).ap()
        counts_d = nc.dram_tensor("counts_d", [2, 128, T, N], BF16).ap()

        keep = allocator(ctx)
        eps_t = keep("eps_t", [128, 1], F32)
        ident = keep("ident", [128, 128], F32)
        ones = keep("ones", [P, 1], F32)
        flag_i = keep("flag_i", [1, 1], I32)
        range_row = keep("range_row", [1, 2 * NW + 1], I32)
        iota_e = keep("iota_e", [P, NE], F32)
        Wg_sb = keep("Wg_sb", [128, KC, NE], F32)
        logits = keep("logits", [P, T, NE], F32)
        top = keep("top", [P, T, 8], F32)
        topi = keep("topi", [P, T, 8], U32)

        graph = ExitStack()
        sb = allocator(graph)
        xn_hi = sb("xn_hi", [P, T, D], F16)
        xn_lo = sb("xn_lo", [P, T, D], F16)
        general = ExitStack()
        gb = allocator(general)
        key_all = gb("key_all", [128, ROWS], F32)
        lo_all = gb("lo_all", [128, ROWS], F32)
        gen_key = gb("gen_key", [128, MW], F16)
        gen_lo = gb("gen_lo", [128, 128], F16)
        gen_counts = gb("gen_counts", [128, 2, T, W], BF16)
        general.close()
        counts = sb("counts", [128, 2, T, GN], BF16)
        gather = ExitStack()
        slot_rows = allocator(gather)("slot_rows", [NW, KS, 2 * CH], F32)
        dst_next = allocator(gather)("dst_next", [P, 2, CPP * CH], I32)
        gather.close()
        hot_key = sb("hot_key", [128, RING, KS, MW], F16)
        hot_lo = sb("hot_lo", [128, RING, 128, KP], F16)
        W1_hi, W1_lo, W2_hi, W2_lo = (sb(n, [128, KC, D], F32R) for n in ("W1_hi", "W1_lo", "W2_hi", "W2_lo"))
        b1_col = sb("b1_col", [128, KC], F32)
        b2_row = sb("b2_row", [P, D], F32)
        key_w = sb("key_w", [128, KS, NW], F32)
        lo_w = sb("lo_w", [128, NW, KP], F16)
        iota_key = sb("iota_key", [128, MW], F16)
        iota_lo = sb("iota_lo", [128, 128, KP], F16)
        win_base = sb("win_base", [128, NW], F32)
        self_row = sb("self_row", [128, 255], F16)
        self_cols = sb("self_cols", [128, MW], F16)

        early = ExitStack()
        sb = allocator(early)
        x_in = sb("x_in", [P, 4, D], F32)
        xn = sb("xn", [P, 2, D], F32)
        stat1 = sb("stat1", [P, T, 6], F32)
        mv1 = sb("mv1", [P, T, 2], F32)
        std1 = sb("std1", [P, T], F32)
        rstd1 = sb("rstd1", [P, T], F32)
        W_raw = sb("W_raw", [128, KC, D], F32)
        dst_i = sb("dst_i", [P, CPP * CH], I32)
        src_i = sb("src_i", [P, CPP * CH], I32)
        edge_a = sb("edge_a", [P, CPP, CH], F32)
        edge_rows_sb = sb("edge_rows_sb", [P, CPP, 2, CH], F32)
        pad_rows = sb("pad_rows", [ROWS - NCH, 2 * CH], F32)
        spans = sb("spans", [P, 2, CPP], F32)
        spans_b = sb("spans_b", [NW, 2, NCH], F32)
        hit = sb("hit", [NW, 2, NCH], F32)
        chunk_up = sb("chunk_up", [NW, NCH], F32)
        chunk_down = sb("chunk_down", [NW, NCH], F32)
        win_lo = sb("win_lo", [NW, 1], F32)
        win_hi = sb("win_hi", [NW, 1], F32)
        first = sb("first", [NW, 2], F32)
        span_i = sb("span_i", [NW, 2], I32)
        flaw = sb("flaw", [P, 4], F32)
        slot_iota = sb("slot_iota", [NW, KS], F32)
        slot_i = sb("slot_i", [NW, KS], I32)
        early.close()

        late = ExitStack()
        sb = allocator(late)
        hT_hi = sb("hT_hi", [128, KC, GN], F32R)
        hT_lo = sb("hT_lo", [128, KC, GN], F32R)
        h1 = sb("h1", [128, 2, GN], F32)
        h1_hi = sb("h1_hi", [128, KC, GN], F32R)
        h1_lo = sb("h1_lo", [128, KC, GN], F32R)
        x_res = sb("x_res", [P, 2, D], F32)
        x2 = sb("x2", [P, 2, D], F32)
        xt = sb("xt", [P, 4, D], F32)
        ln2 = sb("ln2", [P, 2, 10], F32)
        late.close()
        graph.close()

        ffn = ExitStack()
        sb = allocator(ffn)
        w1_hi, w1_lo = (sb(n, [128, NE, KC, H], F32R) for n in ("w1_hi", "w1_lo"))
        w2_hi, w2_lo = (sb(n, [128, NE, HC, D], F32R) for n in ("w2_hi", "w2_lo"))
        w_raw = sb("w_raw", [128, 2, 2, KC * H], F32)
        eb1_col = sb("eb1_col", [128, NE * HC], F32)
        eb2_sb = sb("eb2_sb", [NE, D], F32)
        dest_i = sb("dest_i", [P, 2 * T], I32)
        token_i = sb("token_i", [128, NT], I32)
        expert_i = sb("expert_i", [1, NB], I32)
        end_i = sb("end_i", [1, NE], I32)
        chosen = sb("chosen", [P, 2, T, NE], F32)
        shifted = sb("shifted", [P, T, NE], F32)
        total = sb("total", [P, T], F32)
        share = sb("share", [P, 2, T], F32)
        share_sum = sb("share_sum", [P, T], F32)
        scores = sb("scores", [P, T, NE], F32)
        scores_T = sb("scores_T", [NE, T, P], F32)

        route = ExitStack()
        sb = allocator(route)
        before = sb("before", [P, P], F16)
        ones16 = sb("ones16", [P, P], F16)
        topf = sb("topf", [P, 2, T], F32)
        either = sb("either", [P, T, NE], F16)
        goes_on = sb("goes_on", [P, NE, T], F32)
        tile_count = sb("tile_count", [P, NE, T], F32)
        count_up = sb("count_up", [P, NE, T], F32)
        slot_of = sb("slot_of", [P, NE, T], F32)
        blocks = sb("blocks", [P, NE], F32)
        block_end = sb("block_end", [P, NE], F32)
        block_base = sb("block_base", [P, NE], F32)
        picked = sb("picked", [P, 2, T, NE], F32)
        dest = sb("dest", [P, 2 * T], F32)
        dest_tile = sb("dest_tile", [P, 2 * T], F32)
        dest_tile16 = sb("dest_tile16", [P, 2 * T], F16)
        dest_row = sb("dest_row", [P, 2 * T], F16)
        iota_128 = sb("iota_128", [P, 128], F16)
        iota_nt = sb("iota_nt", [P, NT], F16)
        iota_n = sb("iota_n", [P, 2, T], F16)
        iota_p = sb("iota_p", [P, 1], F32)
        iota_k = sb("iota_k", [1, NB], F32)
        at_row = sb("at_row", [P, 2 * T, 128], F16)
        at_tile = sb("at_tile", [P, 2 * T, NT], F16)
        token_part = sb("token_part", [P, 2 * T, 2, NT], F16)
        token_low = sb("token_low", [128, NT], F32)
        ends_before = sb("ends_before", [1, NB, NE], F32)
        expert_f = sb("expert_f", [1, NB], F32)
        route.close()

        work = ExitStack()
        sb = allocator(work)
        xg = sb("xg", [128, 2, 2, D], F32)
        x_now = sb("x_now", [128, 2, D], F32)
        xT_hi, xT_lo = (sb(n, [128, KC, B], F32R) for n in ("xT_hi", "xT_lo"))
        he = sb("he", [128, HC, B], F32)
        he_hi, he_lo = (sb(n, [128, HC, B], F32R) for n in ("he_hi", "he_lo"))
        y = sb("y", [128, 2, 2, D], F32)
        work.close()

        join = ExitStack()
        sb = allocator(join)
        y_back = sb("y_back", [P, 4, 2, D], F32)
        x2_back = sb("x2_back", [P, 4, D], F32)
        join.close()
        ffn.close()

        psum = ctx.enter_context(nc.psum_tensor("psum", [128, 8, 512], F32))
        WIN, AGG, SM = 0, 2, 6

        names = (
            "dst_in src_in next_blank next_in x_in_a x_in_b x_in_c x_in_d w1_in w2_in small_in tables spans_ready keys_ready "
            "spans_out spans_in rows_out idx_ready gathered rows_turned rows_used stats_ready std_ready xn_ready xn_hi_ready "
            "xn_lo_ready w_split flaws_ready flaws_done range_ready range_out range_in "
            "gen_cleared gen_turned gen_taken gen_free gen_ready gen_win gen_half gen_split gen_stored gen_saved counts_in rest_in "
            "hot_ready win_done counts_ready counts_final agg_main agg_done hT_hi_ready hT_ready mlp1_done relu_ready h1_split "
            "mlp2_done x2_ready std2_ready xt_ready res_in_a res_in_b res_sum x2_out_a x2_out_b xt_turned xt_T_ready gate_done "
            "gate_taken top_ready topi_ready dve_step act_step pool_step "
            "x2_landed route_tables chosen_ready ranked slots_known spread_ready spread_done tokens_ready shifted_ready exp_ready "
            "scores_ready scores_turned scores_T_ready "
            "ew_in_a ew_in_b w_hi_ready w_lo_ready eb_in xg_in_a xg_in_b x_now_ready turned xT_hi_ready xT_ready up_done "
            "gelu_ready he_ready down_done y0_taken y1_taken y_out_a y_out_b yb_in_a yb_in_b yb_in_c yb_in_d "
            "xb_in_a xb_in_b xb_in_c xb_in_d bias_done summed out_a out_b out_c out_d").split()
        S = {n: sem(n) for n in names}

        block = ctx.enter_context(nc.Block())
        x_tiles = x.rearrange("(p t) d -> p t d", t=T)
        x_in_sems = [S["x_in_a"], S["x_in_b"], S["x_in_c"], S["x_in_d"]]
        res_in = [S["res_in_a"], S["res_in_b"]]
        x2_out = [S["x2_out_a"], S["x2_out_b"]]
        ew_in = [S["ew_in_a"], S["ew_in_b"]]
        xg_in = [S["xg_in_a"], S["xg_in_b"]]
        y_out = [S["y_out_a"], S["y_out_b"]]
        yb_in = [S["yb_in_" + c] for c in "abcd"]
        xb_in = [S["xb_in_" + c] for c in "abcd"]
        out_done = [S["out_" + c] for c in "abcd"]

        def stepper(eng, s):
            count = [0]

            def step(ins):
                ins.then_inc(s, 1)
                count[0] += 1
                eng.wait_ge(s, count[0])
            return step

        def mlp1_chunks(part):
            return {0: (0, 1), 1: (2, 3)}.get(part, ())

        def mlp2_tiles(part):
            return {3: (0, 1), 4: (2, 3)}.get(part, ())

        @block.sync
        def _(sp):
            sp.dma_start(dst_i[:], dst.rearrange("(p e) -> p e", p=P)).then_inc(S["dst_in"], 16)
            sp.dma_start(src_i[:], src.rearrange("(p e) -> p e", p=P)).then_inc(S["src_in"], 16)
            sp.wait_ge(S["next_blank"], 1)
            row = CPP * CH
            for n, ahead in enumerate((1, FULL)):
                sp.dma_start(dst_next[0:P - 1, n], dst[ahead:ahead + (P - 1) * row].rearrange("(p e) -> p e", e=row))\
                  .then_inc(S["next_in"], 16)
                sp.dma_start(dst_next[P - 1:P, n, 0:row - ahead], dst[ahead + (P - 1) * row:E].rearrange("(o e) -> o e", o=1))\
                  .then_inc(S["next_in"], 16)
            for t in range(T):
                if t == 4:
                    sp.wait_ge(S["spans_ready"], 1)
                    sp.dma_start(spans_d.rearrange("a (p c) -> p a c", p=P), spans[:]).then_inc(S["spans_out"], 16)
                    sp.wait_ge(S["tables"], 1)
                    sp.dma_start(edge_rows[NCH:ROWS, :], pad_rows[:]).then_inc(S["rows_out"], 16)
                    sp.wait_ge(S["keys_ready"], 1)
                    sp.dma_start(edge_rows[0:NCH, :].rearrange("(p c) e -> p (c e)", p=P),
                                 edge_rows_sb[:].rearrange("p c a e -> p (c a e)")).then_inc(S["rows_out"], 16)
                    sp.wait_ge(S["spans_out"], 16)
                    sp.dma_start(spans_b[:], spans_d.rearrange("(o a) c -> o a c", o=1).broadcast_to([NW, 2, NCH])).then_inc(S["spans_in"], 16)
                if t >= 4:
                    sp.wait_ge(S["xn_ready"], t - 3)
                sp.dma_start(x_in[:, t % 4], x_tiles[:, t]).then_inc(x_in_sems[t % 4], 16)
            sp.wait_ge(S["range_ready"], 2)
            sp.dma_start(range_d[0, 0:2 * NW].rearrange("(w a) -> w a", a=2), span_i[:]).then_inc(S["range_out"], 16)
            sp.dma_start(range_d[:, 2 * NW:], flag_i[:]).then_inc(S["range_out"], 16)
            sp.wait_ge(S["range_out"], 32)
            sp.dma_start(range_row[:], range_d[:, :]).then_inc(S["range_in"], 16)
            sp.wait_ge(S["range_in"], 16)
            flag = sp.value_load(range_row[0:1, 2 * NW:], min_val=0, max_val=1)

            with sp.If(flag > 0):
                sp.sem_inc(S["gen_stored"], 1)
                with sp.Fori(0, NW) as w:
                    sp.wait_ge(S["gen_split"], w + 1)
                    for n in range(2):
                        sp.dma_start(counts_d[n, :, :, bass.ds(w * W, W)], gen_counts[:, n]).then_inc(S["gen_saved"], 16)
                    sp.wait_ge(S["gen_saved"], (w + 1) * 32)
                    sp.sem_inc(S["gen_stored"], 1)

            def store(g, tiles):
                for q in tiles:
                    n = 4 * g + q
                    rows = slice(n * P, (n + 1) * P)
                    sp.wait_ge(S["xt_ready"], n + 1)
                    sp.dma_start(x2_d[rows, :], x2[:, q % 2]).then_inc(x2_out[q % 2], 16)
                    sp.dma_start(xt_d[rows, :], xt[:, q]).then_inc(x2_out[q % 2], 16)

            def group_counts(n, g):
                return counts[:, g % 2], counts_d[n, :, :, g * GN:(g + 1) * GN]

            for it in range(G + 3):
                if 0 <= it - 3:
                    store(it - 3, (2, 3))
                if 0 <= it - 2 < G:
                    store(it - 2, (0, 1))
                if 0 <= it - 1 < G:
                    with sp.If(flag > 0):
                        sp.wait_ge(S["agg_main"], it)
                        sp.dma_start(*group_counts(1, it - 1)).then_inc(S["rest_in"], 16)
                if it < G:
                    sp.wait_ge(S["counts_ready"], WG * (it + 1))
                    with sp.If(flag > 0):
                        sp.dma_start(*group_counts(0, it)).then_inc(S["counts_in"], 16)
                        sp.wait_ge(S["counts_in"], 16 * (it + 1))
                    sp.sem_inc(S["counts_final"], 1)
            for b in range(2):
                sp.wait_ge(x2_out[b], 32 * 2 * G)
            sp.sem_inc(S["x2_landed"], 1)

            def load_expert(e):
                if e >= 2:
                    sp.wait_ge(S["w_hi_ready"], e - 1)
                    sp.wait_ge(S["w_lo_ready"], e - 1)
                sp.dma_start(w_raw[:, e % 2, 0].rearrange("p (k h) -> p k h", k=KC),
                             eW1[e].rearrange("(k p) h -> p k h", p=128)).then_inc(ew_in[e % 2], 16)
                sp.dma_start(w_raw[:, e % 2, 1].rearrange("p (k h) -> p k h", k=HC),
                             eW2[e].rearrange("(k p) h -> p k h", p=128)).then_inc(ew_in[e % 2], 16)

            def load_back(n):
                if n >= 4:
                    sp.wait_ge(out_done[n % 4], 16 * (n // 4))
                sp.dma_start(x2_back[:, n % 4], x2_d[n * P:(n + 1) * P, :]).then_inc(xb_in[n % 4], 16)

            load_expert(0)
            load_expert(1)
            sp.dma_start(eb1_col[:], eb1.rearrange("e (k p) -> p (e k)", p=128), allow_slow_non_contiguous=True).then_inc(S["eb_in"], 16)
            sp.dma_start(eb2_sb[:], eb2[:, :]).then_inc(S["eb_in"], 16)
            for k in range(NB):
                if k + 2 < NE:
                    load_expert(k + 2)
                sp.wait_ge(S["y0_taken"], k + 2)
                sp.wait_ge(S["y1_taken"], k + 2)
                sp.dma_start(y_d[k * B:(k + 1) * B, :].rearrange("(i p) d -> p i d", p=128), y[:, k % 2]).then_inc(y_out[k % 2], 16)
            for n in range(4):
                load_back(n)
            for n in range(T):
                sp.wait_ge(S["summed"], n + 1)
                sp.dma_start(out[n * P:(n + 1) * P, :], x2_back[:, n % 4]).then_inc(out_done[n % 4], 16)
                if n + 4 < T:
                    load_back(n + 4)
            for b in range(4):
                sp.wait_ge(out_done[b], 16 * (T // 4))

        @block.gpsimd
        def _(pool):
            step = stepper(pool, S["pool_step"])
            small = dict(allow_small_or_imprecise_dtypes=True)
            pool.memset(dst_next[:, 0], N)
            pool.memset(dst_next[:, 1], -1).then_inc(S["next_blank"], 1)
            pool.memset(ones[:], 1.0)
            pool.iota(chunk_up[:], pattern=[[1, NCH]], base=1, channel_multiplier=0, **small)
            pool.iota(chunk_down[:], pattern=[[-1, NCH]], base=NCH, channel_multiplier=0, **small)
            pool.iota(win_lo[:], pattern=[[0, 1]], base=0, channel_multiplier=W, **small)
            pool.iota(win_hi[:], pattern=[[0, 1]], base=W - 1, channel_multiplier=W, **small)
            pool.iota(slot_iota[:], pattern=[[1, KS]], base=0, channel_multiplier=0, **small)
            pool.memset(pad_rows[:, 0:CH], FAR)
            pool.memset(pad_rows[:, CH:2 * CH], -1.0).then_inc(S["tables"], 1)
            pool.memset(ident[:], 0.0)
            pool.memset(eps_t[:], EPS)
            pool.iota(iota_e[:], pattern=[[1, NE]], base=0, channel_multiplier=0, **small)
            pool.memset(lo_w[:], -1.0)
            pool.memset(self_row[:], 0.0)
            step(pool.memset(self_cols[:], 0.0))
            pool.affine_select(out=ident[:], in_=ident[:], compare_op=ALU.not_equal, fill=1.0, base=0,
                               pattern=[[-1, 128]], channel_multiplier=1)
            pool.affine_select(out=self_row[:], in_=self_row[:], compare_op=ALU.not_equal, fill=1.0, base=127,
                               pattern=[[-1, 255]], channel_multiplier=1000)
            cols = self_cols[:].rearrange("p (w h) -> p w h", w=W)
            pool.affine_select(out=cols, in_=cols, compare_op=ALU.not_equal, fill=1.0, base=0,
                               pattern=[[1, W], [-1, T]], channel_multiplier=0)
            pool.iota(iota_key[:], pattern=[[1, MW]], base=0, channel_multiplier=0, **small)
            pool.iota(iota_lo[:], pattern=[[1, 128], [0, KP]], base=0, channel_multiplier=0, **small)
            pool.iota(win_base[:], pattern=[[MW, NW]], base=0, channel_multiplier=0, **small).then_inc(S["tables"], 1)

            def low_parts(a, b):
                for t in range(a, b):
                    pool.wait_ge(S["xn_hi_ready"], t + 1)
                    pool.tensor_tensor(xn_lo[:, t], xn[:, t % 2], xn_hi[:, t], ALU.subtract).then_inc(S["xn_lo_ready"], 1)

            low_parts(0, LOOK)
            pool.wait_ge(S["idx_ready"], 1)
            pool.wait_ge(S["rows_out"], 32)
            for k in range(KS):
                pool.indirect_dma_start(out=slot_rows[:, k], out_offset=None, in_=edge_rows[:, :],
                                        in_offset=bass.IndirectOffsetOnAxis(ap=slot_i[:, k:k + 1], axis=0),
                                        bounds_check=ROWS - 1).then_inc(S["gathered"], 16)
            low_parts(LOOK, T)
            for n, (hi, lo, s) in enumerate(((W1_hi, W1_lo, S["w1_in"]), (W2_hi, W2_lo, S["w2_in"]))):
                pool.wait_ge(s, 16)
                step(pool.tensor_copy(hi[:], W_raw[:]))
                pool.tensor_tensor(lo[:], W_raw[:], hi[:].bitcast(F32), ALU.subtract).then_inc(S["w_split"], 1)

            pool.wait_ge(S["small_in"], 48)
            for g in range(G):
                for m in range(KC):
                    pool.wait_ge(S["relu_ready"], 4 * g + m + 1)
                    if m == 0 and g >= 1:
                        pool.wait_ge(S["mlp2_done"], 4 * g)
                    step(pool.tensor_copy(h1_hi[:, m], h1[:, m % 2]))
                    pool.tensor_tensor(h1_lo[:, m], h1[:, m % 2], h1_hi[:, m].bitcast(F32), ALU.subtract)\
                        .then_inc(S["h1_split"], 1)
                for q in range(4):
                    pool.wait_ge(res_in[q % 2], 16 * (2 * g + q // 2 + 1))
                    pool.tensor_tensor(x_res[:, q % 2], x_res[:, q % 2], b2_row[:], ALU.add).then_inc(S["res_sum"], 1)

            pool.wait_ge(S["x2_landed"], 1)
            pool.iota(iota_128[:], pattern=[[1, 128]], base=0, channel_multiplier=0, **small)
            pool.iota(iota_nt[:], pattern=[[1, NT]], base=0, channel_multiplier=0, **small)
            pool.iota(iota_n[:], pattern=[[0, 2], [1, T]], base=0, channel_multiplier=0, **small)
            pool.iota(iota_p[:], pattern=[[0, 1]], base=0, channel_multiplier=1, **small)
            pool.iota(iota_k[:], pattern=[[1, NB]], base=0, channel_multiplier=0, **small)
            pool.memset(ones16[:], 1.0)
            pool.memset(before[:], 1.0)
            step(pool.memset(goes_on[:], 1.0))
            pool.affine_select(out=before[:], in_=before[:], compare_op=ALU.is_gt, fill=0.0, base=0,
                               pattern=[[1, P]], channel_multiplier=-1)
            pool.affine_select(out=goes_on[:], in_=goes_on[:], compare_op=ALU.is_gt, fill=0.0, base=0,
                               pattern=[[0, NE], [1, T]], channel_multiplier=0).then_inc(S["route_tables"], 1)

            def split_low(e):
                pool.wait_ge(ew_in[e % 2], 32 * (e // 2 + 1))
                pool.wait_ge(S["w_hi_ready"], e + 1)
                pool.tensor_tensor(w1_lo[:, e], w_raw[:, e % 2, 0], w1_hi[:, e].bitcast(F32), ALU.subtract)
                pool.tensor_tensor(w2_lo[:, e], w_raw[:, e % 2, 1], w2_hi[:, e].bitcast(F32), ALU.subtract)\
                    .then_inc(S["w_lo_ready"], 1)

            def gather(k):
                if k >= 2:
                    pool.wait_ge(S["x_now_ready"], k - 1)
                for i in range(2):
                    pool.indirect_dma_start(out=xg[:, k % 2, i], out_offset=None, in_=xt_d[:, :],
                                            in_offset=bass.IndirectOffsetOnAxis(ap=token_i[:, 2 * k + i:2 * k + i + 1], axis=0),
                                            bounds_check=N - 1).then_inc(xg_in[k % 2], 16)

            split_low(0)
            split_low(1)
            pool.wait_ge(S["tokens_ready"], 1)
            for k in range(NB + 1):
                gather(k)
                if 2 <= k < NE:
                    split_low(k)
            for b in range(2):
                pool.wait_ge(y_out[b], 16 * ((NB + 1 - b) // 2))
            for n in range(T):
                if n >= 4:
                    pool.wait_ge(S["summed"], n - 3)
                for c in range(2):
                    pool.indirect_dma_start(out=y_back[:, n % 4, c], out_offset=None, in_=y_d[:, :],
                                            in_offset=bass.IndirectOffsetOnAxis(ap=dest_i[:, c * T + n:c * T + n + 1], axis=0),
                                            bounds_check=NB * B - 1).then_inc(yb_in[n % 4], 16)

        @block.scalar
        def _(act):
            step = stepper(act, S["act_step"])
            for n, (raw, s) in enumerate(((gW1, S["w1_in"]), (gW2, S["w2_in"]))):
                if n:
                    act.wait_ge(S["w_split"], 1)
                act.dma_start(W_raw[:], raw.rearrange("(k p) n -> p k n", p=128)).then_inc(s, 16)
                if n == 0:
                    act.dma_start(Wg_sb[:], Wg.rearrange("(k p) e -> p k e", p=128)).then_inc(S["small_in"], 16)
                    act.dma_start(b1_col[:], gb1.rearrange("(k p) -> p k", p=128), allow_slow_non_contiguous=True).then_inc(S["small_in"], 16)
                    act.dma_start(b2_row[:], gb2.rearrange("(o n) -> o n", o=1).broadcast_to([P, D])).then_inc(S["small_in"], 16)
                    act.wait_ge(S["tables"], 2)
                    for t in range(T):
                        act.wait_ge(S["stats_ready"], t + 1)
                        act.activation(std1[:, t:t + 1], mv1[:, t, 1:2], ACT.Sqrt, bias=eps_t[0:P, 0:1]).then_inc(S["std_ready"], 1)
                        if t >= 1:
                            act.wait_ge(S["xn_ready"], t)
                            act.activation(xn_hi[:, t - 1], xn[:, (t - 1) % 2], ACT.Copy).then_inc(S["xn_hi_ready"], 1)
                    act.wait_ge(S["xn_ready"], T)
                    act.activation(xn_hi[:, T - 1], xn[:, (T - 1) % 2], ACT.Copy).then_inc(S["xn_hi_ready"], 1)

            act.wait_ge(S["small_in"], 48)

            def load_residual(g, q):
                n = 4 * g + q
                if n >= 2:
                    act.wait_ge(S["x2_ready"], n - 1)
                act.dma_start(x_res[:, q % 2], x[n * P:(n + 1) * P, :]).then_inc(res_in[q % 2], 16)

            def std2s(g, tiles):
                for q in tiles:
                    act.wait_ge(S["x2_ready"], 4 * g + q + 1)
                    act.activation(ln2[:, q % 2, 8:9], ln2[:, q % 2, 7:8], ACT.Sqrt, bias=eps_t[0:P, 0:1])\
                       .then_inc(S["std2_ready"], 1)
                    if q < 2:
                        load_residual(g, q + 2)

            def gate_rows(g, tiles):
                for q in tiles:
                    n = 4 * g + q
                    act.wait_ge(S["xt_turned"], n + 1)
                    if q == 0 and g + 1 < G:
                        act.wait_ge(S["h1_split"], 4 * (g + 2))
                    if q >= 2:
                        act.wait_ge(S["gate_done"], n - 1)
                    act.activation(h1[:, q % 2], psum[:, SM + q % 2, 0:KC * P], ACT.Copy).then_inc(S["xt_T_ready"], 1)

            for it in range(G + 3):
                g = it - 2
                for part in range(PARTS):
                    if 0 <= g < G and part == 0:
                        if g == 0:
                            act.wait_ge(S["w_split"], 2)
                        act.wait_ge(S["agg_done"], g + 1)
                        for c in range(KC):
                            if c == 0 and g >= 1:
                                act.wait_ge(S["mlp1_done"], 4 * g)
                            act.activation(hT_hi[:, c], psum[:, AGG + c, 0:GN], ACT.Copy).then_inc(S["hT_hi_ready"], 1)
                    if part == 0 and 0 <= g - 1 < G:
                        std2s(g - 1, (2, 3))
                    if part == 4 and 0 <= g < G:
                        std2s(g, (0, 1))
                    for j in range(WP):
                        if it < G:
                            w = WG * it + WP * part + j
                            act.wait_ge(S["win_done"], w + 1)
                            if part == 0 and j == 0 and it >= 2:
                                act.wait_ge(S["agg_done"], it - 1)
                            place = W * (WP * part + j)
                            act.activation(counts[:, it % 2, :, place:place + W],
                                           psum[:, WIN + j % 2, 0:MW].rearrange("p (w h) -> p h w", w=W),
                                           ACT.Copy).then_inc(S["counts_ready"], 1)
                        if 0 <= it - 3 and (part, j) == (2, 2):
                            gate_rows(it - 3, (0, 1))
                        if 0 <= it - 3 and (part, j) == (3, 0):
                            gate_rows(it - 3, (2, 3))
                    if 0 <= g < G:
                        for m in mlp1_chunks(part):
                            act.wait_ge(S["mlp1_done"], 4 * g + m + 1)
                            if 4 * g + m >= 2:
                                act.wait_ge(S["h1_split"], 4 * g + m - 1)
                            if m < 2 and g >= 2:
                                act.wait_ge(S["gate_done"], 4 * (g - 1))
                            act.activation(h1[:, m % 2], psum[:, SM + m % 2, 0:GN], ACT.Relu, bias=b1_col[:, m:m + 1])\
                               .then_inc(S["relu_ready"], 1)
                        if part == 2:
                            load_residual(g, 0)
                            load_residual(g, 1)

            def split_high(e):
                act.wait_ge(ew_in[e % 2], 32 * (e // 2 + 1))
                act.activation(w1_hi[:, e], w_raw[:, e % 2, 0], ACT.Copy)
                act.activation(w2_hi[:, e], w_raw[:, e % 2, 1], ACT.Copy).then_inc(S["w_hi_ready"], 1)

            act.wait_ge(S["x2_landed"], 1)
            act.wait_ge(S["shifted_ready"], 1)
            act.activation(shifted[:], shifted[:], ACT.Exp)
            act.activation(share[:], share[:], ACT.Exp).then_inc(S["exp_ready"], 1)
            split_high(0)
            split_high(1)

            def take_block(k):
                act.wait_ge(xg_in[k % 2], 32 * (k // 2 + 1))
                if k >= 1:
                    act.wait_ge(S["turned"], 2 * k)
                act.activation(x_now[:], xg[:, k % 2], ACT.Copy).then_inc(S["x_now_ready"], 1)

            def turned_high(k):
                for i in range(2):
                    act.wait_ge(S["turned"], 2 * k + i + 1)
                    act.activation(xT_hi[:, :, i * 128:(i + 1) * 128], psum[:, i].rearrange("p (c n) -> p c n", c=KC), ACT.Copy)\
                       .then_inc(S["xT_hi_ready"], 1)

            take_block(0)
            turned_high(0)
            take_block(1)
            act.wait_ge(S["eb_in"], 32)
            act.wait_ge(S["slots_known"], 1)
            act.sem_inc(S["y1_taken"], 1)
            for k in range(NB):
                expert = act.value_load(expert_i[0:1, k:k + 1], min_val=0, max_val=NE - 1)
                for m in range(HC):
                    act.wait_ge(S["up_done"], HC * k + m + 1)
                    if k >= 1:
                        act.wait_ge(S["he_ready"], HC * (k - 1) + m + 1)
                    act.activation(he[:, m], psum[:, 2 + m, 0:B], ACT.Gelu, bias=eb1_col[:, bass.ds(expert * HC + m, 1)])\
                       .then_inc(S["gelu_ready"], 1)
                turned_high(k + 1)
                if k + 2 <= NB:
                    take_block(k + 2)
                if k + 2 < NE:
                    split_high(k + 2)
                act.wait_ge(S["down_done"], 2 * k + 2)
                if k >= 2:
                    act.wait_ge(y_out[k % 2], 16 * (k // 2))
                act.activation(y[:, k % 2, 1], psum[:, 5], ACT.Copy).then_inc(S["y1_taken"], 1)

        @block.vector
        def _(dve):
            step = stepper(dve, S["dve_step"])
            key_part, lo_part = edge_rows_sb[:, :, 0], edge_rows_sb[:, :, 1]
            dve.wait_ge(S["dst_in"], 16)
            dst_v = dst_i[:].rearrange("p (c e) -> p c e", c=CPP)
            src_v = src_i[:].rearrange("p (c e) -> p c e", c=CPP)
            dve.tensor_reduce(spans[:, 0], dst_v, AX.X, ALU.min)
            dve.tensor_reduce(spans[:, 1], dst_v, AX.X, ALU.max).then_inc(S["spans_ready"], 1)
            dve.wait_ge(S["src_in"], 16)
            step(dve.tensor_scalar(lo_part, src_v, 1.0 / T, 0.5 / T - 0.5, ALU.mult, ALU.add))
            step(dve.tensor_scalar(lo_part, lo_part, ROUND, ROUND, ALU.add, ALU.subtract))
            step(dve.scalar_tensor_tensor(edge_a[:], lo_part, -float(T), src_v, ALU.mult, ALU.add))
            dve.scalar_tensor_tensor(key_part, dst_v, float(T), edge_a[:], ALU.mult, ALU.add).then_inc(S["keys_ready"], 1)

            def normalise(t):
                dve.wait_ge(x_in_sems[t % 4], 16 * (t // 4 + 1))
                step(dve.bn_stats(stat1[:, t], x_in[:, t % 4]))
                dve.bn_aggr(mv1[:, t], stat1[:, t]).then_inc(S["stats_ready"], 1)

            def normalise_end(t):
                dve.wait_ge(S["std_ready"], t + 1)
                step(dve.reciprocal(rstd1[:, t:t + 1], std1[:, t:t + 1]))
                if t >= 2:
                    dve.wait_ge(S["xn_lo_ready"], t - 1)
                ins = dve.tensor_scalar(xn[:, t % 2], x_in[:, t % 4], mv1[:, t, 0:1], rstd1[:, t:t + 1],
                                        ALU.subtract, ALU.mult)
                ins.then_inc(S["xn_ready"], 1)

            def find_windows():
                dve.wait_ge(S["tables"], 1)
                dve.wait_ge(S["spans_in"], 16)
                step(dve.tensor_scalar(hit[:, 0], spans_b[:, 0], win_hi[:], None, ALU.is_le))
                step(dve.scalar_tensor_tensor(hit[:, 0], spans_b[:, 1], win_lo[:], hit[:, 0], ALU.is_ge, ALU.mult))
                step(dve.tensor_tensor(hit[:, 1], hit[:, 0], chunk_down[:], ALU.mult))
                step(dve.tensor_reduce(first[:, 0:1], hit[:, 1], AX.X, ALU.max))
                step(dve.tensor_scalar(first[:, 1:2], first[:, 0:1], -1.0, float(NCH), ALU.mult, ALU.add))
                dve.tensor_scalar(slot_i[:], slot_iota[:], first[:, 1:2], None, ALU.add).then_inc(S["idx_ready"], 1)
                step(dve.tensor_tensor(hit[:, 1], hit[:, 0], chunk_up[:], ALU.mult))
                step(dve.tensor_reduce(first[:, 0:1], hit[:, 1], AX.X, ALU.max))
                step(dve.tensor_copy(span_i[:, 0:1], first[:, 1:2]))
                step(dve.scalar_tensor_tensor(span_i[:, 1:2], first[:, 1:2], 1.0, first[:, 0:1], ALU.add, ALU.max))
                step(dve.scalar_tensor_tensor(flaw[:, 0:1], first[:, 1:2], float(KS), first[:, 0:1], ALU.add, ALU.is_lt))
                dve.wait_ge(S["next_in"], 64)
                for n, op in enumerate((ALU.is_gt, ALU.is_equal)):
                    step(dve.tensor_tensor(edge_a[:].rearrange("p c e -> p (c e)"), dst_i[:], dst_next[:, n], op))
                    step(dve.tensor_reduce(flaw[:, n + 1:n + 2], edge_a[:], AX.XY, ALU.max))
                step(dve.tensor_reduce(flaw[:, 3:4], flaw[:, 0:3], AX.X, ALU.add))
                dve.tensor_copy(flaw[:, 0:1], flaw[:, 3:4]).then_inc(S["flaws_ready"], 1)

            def take_rows(k):
                at = 256 * (k % 2)
                dve.tensor_tensor(key_w[:, k], psum[:, AGG + k // 2, at:at + NW], win_base[:], ALU.subtract)
                dve.tensor_copy(lo_w[:, :, k], psum[:, AGG + k // 2, at + 128:at + 128 + NW]).then_inc(S["rows_used"], 1)

            for t in range(T):
                normalise(t)
                if t >= 1:
                    normalise_end(t - 1)
                if t == LOOK:
                    find_windows()
            normalise_end(T - 1)
            dve.wait_ge(S["tables"], 2)
            dve.wait_ge(S["rows_turned"], KS)
            for k in range(KS):
                take_rows(k)
            dve.wait_ge(S["rows_used"], KS)
            dve.wait_ge(S["flaws_done"], 1)
            dve.tensor_scalar(flag_i[:], psum[0:1, SM, 0:1], 1.0, None, ALU.min).then_inc(S["range_ready"], 2)

            dve.wait_ge(S["range_in"], 16)
            flag = dve.value_load(range_row[0:1, 2 * NW:], min_val=0, max_val=1)
            with dve.If(flag > 0):
                dve.memset(key_all[:], FAR)
                dve.memset(lo_all[:], -1.0).then_inc(S["gen_cleared"], 1)
                dve.wait_ge(S["gen_cleared"], 1)
                dve.wait_ge(S["gen_turned"], 1)
                for n, (table, j) in enumerate((table, j) for table in (key_all, lo_all) for j in range(CPP)):
                    place = table[:, 0:NCH].rearrange("p (c j) -> p j c", j=CPP)[:, j]
                    dve.tensor_copy(place, psum[:, AGG + n // 4, 128 * (n % 4):128 * (n % 4) + P]).then_inc(S["gen_taken"], 1)
                dve.wait_ge(S["gen_taken"], 2 * CPP)
                visit = dve.alloc_register("dve_visit")
                dve.reg_mov(visit, 0)
                with dve.Fori(0, NW) as w:
                    start = dve.value_load(range_row[0:1, bass.ds(w * 2, 1)], min_val=0, max_val=NCH)
                    end = dve.value_load(range_row[0:1, bass.ds(w * 2 + 1, 1)], min_val=1, max_val=NCH + 1)
                    with dve.Fori(start, end) as c:
                        n = dve.snap(visit, min_val=0, max_val=NW * NCH)
                        dve.wait_ge(S["gen_free"], n + 1)
                        dve.tensor_scalar(gen_key[:], iota_key[:], win_base[:, bass.ds(w, 1)], key_all[:, bass.ds(c, 1)],
                                          ALU.add, ALU.is_equal)
                        dve.tensor_scalar(gen_lo[:], iota_lo[:, :, 0], lo_all[:, bass.ds(c, 1)], None, ALU.is_equal)\
                           .then_inc(S["gen_ready"], 1)
                        dve.reg_add(visit, visit, 1)
                    dve.wait_ge(S["gen_win"], w + 1)
                    dve.wait_ge(S["gen_stored"], w + 1)
                    window_sum = psum[:, WIN, 0:MW].rearrange("p (w h) -> p h w", w=W)
                    dve.tensor_copy(gen_counts[:, 0], window_sum).then_inc(S["gen_half"], 1)
                    dve.wait_ge(S["gen_half"], w + 1)
                    dve.tensor_tensor(gen_counts[:, 1], window_sum, gen_counts[:, 0], ALU.subtract).then_inc(S["gen_split"], 1)
                dve.wait_ge(S["gen_stored"], NW + 1)

            def one_hots(w):
                if w >= RING:
                    dve.wait_ge(S["win_done"], w - RING + 1)
                for k in range(KS):
                    dve.tensor_scalar(hot_key[:, w % RING, k], iota_key[:], key_w[:, k, w:w + 1], None, ALU.is_equal)
                dve.tensor_tensor(hot_lo[:, w % RING], iota_lo[:],
                                  lo_w[:, w].rearrange("p (o k) -> p o k", o=1).broadcast_to([128, 128, KP]),
                                  ALU.is_equal).then_inc(S["hot_ready"], 1)

            def split_sums(g):
                if g == 0:
                    dve.wait_ge(S["w_split"], 2)
                for c in range(KC):
                    dve.wait_ge(S["hT_hi_ready"], 4 * g + c + 1)
                    dve.tensor_tensor(hT_lo[:, c], psum[:, AGG + c, 0:GN], hT_hi[:, c].bitcast(F32), ALU.subtract)\
                       .then_inc(S["hT_ready"], 1)

            def residual(g, q):
                n = 4 * g + q
                dve.wait_ge(S["mlp2_done"], n + 1)
                dve.wait_ge(S["res_sum"], n + 1)
                if n >= 2:
                    dve.wait_ge(x2_out[q % 2], 32 * (2 * g + q // 2))
                step(dve.tensor_tensor(x2[:, q % 2], psum[0:P, SM + q % 2, :], x_res[:, q % 2], ALU.add))
                step(dve.bn_stats(ln2[:, q % 2, 0:6], x2[:, q % 2]))
                dve.bn_aggr(ln2[:, q % 2, 6:8], ln2[:, q % 2, 0:6]).then_inc(S["x2_ready"], 1)

            def residual_end(g, q):
                n = 4 * g + q
                dve.wait_ge(S["std2_ready"], n + 1)
                if g >= 1:
                    dve.wait_ge(S["xt_turned"], n - 3)
                step(dve.reciprocal(ln2[:, q % 2, 9:10], ln2[:, q % 2, 8:9]))
                dve.tensor_scalar(xt[:, q], x2[:, q % 2], ln2[:, q % 2, 6:7], ln2[:, q % 2, 9:10],
                                  ALU.subtract, ALU.mult).then_inc(S["xt_ready"], 1)

            def gate_take(g, tiles):
                for q in tiles:
                    n = 4 * g + q
                    dve.wait_ge(S["gate_done"], n + 1)
                    dve.tensor_copy(logits[:, n], psum[0:P, SM + q % 2, 0:NE]).then_inc(S["gate_taken"], 1)
                for q in tiles:
                    n = 4 * g + q
                    dve.wait_ge(S["gate_taken"], n + 1)
                    dve.max(top[:, n], logits[:, n]).then_inc(S["top_ready"], 1)
                for q in tiles:
                    n = 4 * g + q
                    dve.wait_ge(S["top_ready"], n + 1)
                    dve.max_index(topi[:, n], top[:, n], logits[:, n]).then_inc(S["topi_ready"], 1)

            for it in range(G + 3):
                g = it - 2
                for part in range(PARTS):
                    for j in range(WP):
                        if it < G:
                            one_hots(WG * it + WP * part + j)
                        if 0 <= it - 3 and (part, j) == (3, 3):
                            gate_take(it - 3, (0, 1))
                        if 0 <= it - 3 and (part, j) == (4, 2):
                            gate_take(it - 3, (2, 3))
                        if j == RING - 1:
                            if part == 0:
                                if 0 <= g < G:
                                    split_sums(g)
                                if 0 <= g - 1 < G:
                                    for q in (2, 3):
                                        residual(g - 1, q)
                                    for q in (2, 3):
                                        residual_end(g - 1, q)
                            elif 0 <= g < G and part == 4:
                                for q in (0, 1):
                                    residual(g, q)
                                for q in (0, 1):
                                    residual_end(g, q)

            def over(ap, shape):
                return ap.broadcast_to(shape)

            dve.wait_ge(S["x2_landed"], 1)
            dve.wait_ge(S["topi_ready"], T)
            step(dve.tensor_copy(topf[:], topi[:, :, 0:2].rearrange("p n c -> p c n")))
            dve.wait_ge(S["route_tables"], 1)
            experts = iota_e[:].rearrange("p (o e) -> p o e", o=1).broadcast_to([P, T, NE])
            for c in range(2):
                ins = dve.tensor_tensor(chosen[:, c], experts, topf[:, c].rearrange("p (n o) -> p n o", o=1).broadcast_to([P, T, NE]),
                                        ALU.is_equal)
            step(ins)
            dve.tensor_tensor(either[:], chosen[:, 0], chosen[:, 1], ALU.add).then_inc(S["chosen_ready"], 1)
            dve.tensor_tensor(shifted[:], logits[:], top[:, :, 0:1].broadcast_to([P, T, NE]), ALU.subtract)
            dve.tensor_tensor(share[:], top[:, :, 0:2].rearrange("p n c -> p c n"),
                              top[:, :, 0:1].rearrange("p n o -> p o n").broadcast_to([P, 2, T]), ALU.subtract)\
               .then_inc(S["shifted_ready"], 1)
            dve.wait_ge(S["ranked"], 1)
            step(dve.tensor_copy(tile_count[:], psum[0:P, 1, 0:T * NE].rearrange("p (n e) -> p e n", e=NE)))
            step(dve.tensor_tensor_scan(count_up[:].rearrange("p e n -> p (e n)"), goes_on[:].rearrange("p e n -> p (e n)"),
                                        tile_count[:].rearrange("p e n -> p (e n)"), 0.0, ALU.mult, ALU.add))
            dve.tensor_tensor(slot_of[:], count_up[:], tile_count[:], ALU.subtract)
            step(dve.tensor_scalar(blocks[:], count_up[:, :, T - 1], 1.0 / B, (B - 1.0) / B - 0.5 + 0.5 / B, ALU.mult, ALU.add))
            step(dve.tensor_scalar(blocks[:], blocks[:], ROUND, ROUND, ALU.add, ALU.subtract))
            step(dve.tensor_scalar(blocks[:], blocks[:], 1.0, None, ALU.max))
            step(dve.tensor_tensor_scan(block_end[:], ones[:].broadcast_to([P, NE]), blocks[:], 0.0, ALU.mult, ALU.add))
            step(dve.tensor_tensor(block_base[:], block_end[:], blocks[:], ALU.subtract))
            step(dve.tensor_tensor(slot_of[:], slot_of[:], psum[0:P, 0, 0:T * NE].rearrange("p (n e) -> p e n", e=NE), ALU.add))
            step(dve.scalar_tensor_tensor(slot_of[:], block_base[:].rearrange("p (e o) -> p e o", o=1).broadcast_to([P, NE, T]),
                                          float(B), slot_of[:], ALU.mult, ALU.add))
            for c in range(2):
                ins = dve.tensor_tensor(picked[:, c], chosen[:, c], slot_of[:].rearrange("p e n -> p n e"), ALU.mult)
            step(ins)
            step(dve.tensor_reduce(dest[:], picked[:].rearrange("p c n e -> p (c n) e"), AX.X, ALU.add))
            step(dve.tensor_scalar(dest_tile[:], dest[:], 1.0 / 128, -0.5 + 0.5 / 128, ALU.mult, ALU.add))
            step(dve.tensor_scalar(dest_tile[:], dest_tile[:], ROUND, ROUND, ALU.add, ALU.subtract))
            dve.tensor_copy(dest_tile16[:], dest_tile[:])
            step(dve.scalar_tensor_tensor(dest_row[:], dest_tile[:], -128.0, dest[:], ALU.mult, ALU.add))
            step(dve.tensor_tensor(at_tile[:], iota_nt[:].rearrange("p (o s) -> p o s", o=1).broadcast_to([P, 2 * T, NT]),
                                   dest_tile16[:].rearrange("p (n o) -> p n o", o=1).broadcast_to([P, 2 * T, NT]), ALU.is_equal))
            dve.tensor_scalar(token_part[:, :, 0], at_tile[:], iota_p[:], None, ALU.mult)
            dve.tensor_tensor(token_part[:, :, 1], at_tile[:],
                              iota_n[:].rearrange("p c (n o) -> p (c n) o", o=1).broadcast_to([P, 2 * T, NT]), ALU.mult)
            dve.tensor_tensor(at_row[:], iota_128[:].rearrange("p (o s) -> p o s", o=1).broadcast_to([P, 2 * T, 128]),
                              dest_row[:].rearrange("p (n o) -> p n o", o=1).broadcast_to([P, 2 * T, 128]), ALU.is_equal)\
               .then_inc(S["spread_ready"], 1)
            step(dve.tensor_tensor(ends_before[:], block_end[0:1].rearrange("p (o e) -> p o e", o=1).broadcast_to([1, NB, NE]),
                                   iota_k[:].rearrange("p (k o) -> p k o", o=1).broadcast_to([1, NB, NE]), ALU.is_le))
            step(dve.tensor_reduce(expert_f[:], ends_before[:], AX.X, ALU.add))
            dve.tensor_scalar(expert_i[:], expert_f[:], float(NE - 1), None, ALU.min)
            dve.tensor_copy(end_i[:], block_end[0:1]).then_inc(S["slots_known"], 1)
            dve.wait_ge(S["spread_done"], 1)
            step(dve.tensor_copy(dest_i[:], dest[:]))
            step(dve.tensor_copy(token_low[:], psum[:, 2, 0:NT]))
            dve.scalar_tensor_tensor(token_i[:], psum[:, 2, NT:2 * NT], float(P), token_low[:], ALU.mult, ALU.add)\
               .then_inc(S["tokens_ready"], 1)
            dve.wait_ge(S["exp_ready"], 1)
            step(dve.tensor_reduce(total[:], shifted[:], AX.X, ALU.add))
            step(dve.reciprocal(total[:], total[:]))
            step(dve.tensor_tensor(share[:], share[:], total[:].rearrange("p (o n) -> p o n", o=1).broadcast_to([P, 2, T]), ALU.mult))
            step(dve.tensor_tensor(share_sum[:], share[:, 0], share[:, 1], ALU.add))
            step(dve.tensor_scalar(share_sum[:], share_sum[:], 1e-6, None, ALU.add))
            step(dve.reciprocal(share_sum[:], share_sum[:]))
            step(dve.tensor_tensor(share[:], share[:], share_sum[:].rearrange("p (o n) -> p o n", o=1).broadcast_to([P, 2, T]), ALU.mult))
            for c in range(2):
                ins = dve.tensor_tensor(chosen[:, c], chosen[:, c], share[:, c].rearrange("p (n o) -> p n o", o=1).broadcast_to([P, T, NE]),
                                        ALU.mult)
            step(ins)
            dve.tensor_tensor(scores[:], chosen[:, 0], chosen[:, 1], ALU.add).then_inc(S["scores_ready"], 1)

            def turned_low(k):
                for i in range(2):
                    dve.wait_ge(S["xT_hi_ready"], 2 * k + i + 1)
                    part = slice(i * 128, (i + 1) * 128)
                    dve.tensor_tensor(xT_lo[:, :, part], psum[:, i].rearrange("p (c n) -> p c n", c=KC),
                                      xT_hi[:, :, part].bitcast(F32), ALU.subtract).then_inc(S["xT_ready"], 1)

            turned_low(0)
            dve.sem_inc(S["y0_taken"], 1)
            for k in range(NB):
                for m in range(HC):
                    dve.wait_ge(S["gelu_ready"], HC * k + m + 1)
                    if k >= 1:
                        dve.wait_ge(S["down_done"], 2 * k)
                    step(dve.tensor_copy(he_hi[:, m], he[:, m]))
                    dve.tensor_tensor(he_lo[:, m], he[:, m], he_hi[:, m].bitcast(F32), ALU.subtract).then_inc(S["he_ready"], 1)
                turned_low(k + 1)
                dve.wait_ge(S["down_done"], 2 * k + 1)
                if k >= 2:
                    dve.wait_ge(y_out[k % 2], 16 * (k // 2))
                dve.tensor_copy(y[:, k % 2, 0], psum[:, 4]).then_inc(S["y0_taken"], 1)

            for n in range(T):
                if n % 4 == 0:
                    dve.wait_ge(S["scores_turned"], n // 4 + 1)
                    dve.tensor_copy(scores_T[:, n:n + 4], psum[0:NE, 0, 0:4 * P].rearrange("p (q n) -> p q n", q=4))\
                       .then_inc(S["scores_T_ready"], 1)
                dve.wait_ge(S["bias_done"], n + 1)
                dve.wait_ge(xb_in[n % 4], 16 * (n // 4 + 1))
                row = x2_back[:, n % 4]
                step(dve.tensor_tensor(row, row, psum[0:P, 1 + n % 2, :], ALU.add))
                dve.wait_ge(yb_in[n % 4], 32 * (n // 4 + 1))
                step(dve.scalar_tensor_tensor(row, y_back[:, n % 4, 0], share[:, 0, n:n + 1], row, ALU.mult, ALU.add))
                dve.scalar_tensor_tensor(row, y_back[:, n % 4, 1], share[:, 1, n:n + 1], row, ALU.mult, ALU.add)\
                   .then_inc(S["summed"], 1)

        @block.tensor
        def _(pe):
            mm = pe.matmul
            pe.wait_ge(S["tables"], 2)
            pe.wait_ge(S["gathered"], 16 * KS)
            for k in range(KS):
                at = 256 * (k % 2)
                pe.transpose(psum[:, AGG + k // 2, at:at + NW], slot_rows[:, k, 0:CH], ident[0:NW, 0:NW])
                pe.transpose(psum[:, AGG + k // 2, at + 128:at + 128 + NW], slot_rows[:, k, CH:2 * CH], ident[0:NW, 0:NW])\
                  .then_inc(S["rows_turned"], 1)

            pe.wait_ge(S["flaws_ready"], 1)
            mm(psum[0:1, SM, 0:1], flaw[:, 0:1], ones[:], start=True, stop=True).then_inc(S["flaws_done"], 1)
            pe.wait_ge(S["range_in"], 16)
            flag = pe.value_load(range_row[0:1, 2 * NW:], min_val=0, max_val=1)
            with pe.If(flag > 0):
                pe.wait_ge(S["rows_used"], KS)
                for n, (v, j) in enumerate((v, j) for v in range(2) for j in range(CPP)):
                    ins = pe.transpose(psum[:, AGG + n // 4, 128 * (n % 4):128 * (n % 4) + P], edge_rows_sb[:, j, v], ident[0:P, 0:P])
                ins.then_inc(S["gen_turned"], 1)
                pe.sem_inc(S["gen_free"], 1)
                visit = pe.alloc_register("pe_visit")
                pe.reg_mov(visit, 0)
                bank = psum[:, WIN, 0:MW]
                with pe.Fori(0, NW) as w:
                    start = pe.value_load(range_row[0:1, bass.ds(w * 2, 1)], min_val=0, max_val=NCH)
                    end = pe.value_load(range_row[0:1, bass.ds(w * 2 + 1, 1)], min_val=1, max_val=NCH + 1)
                    pe.wait_ge(S["gen_stored"], w + 1)
                    mm(bank, self_row[:, bass.ds(w * -1 + 127, 128)], self_cols[:], start=True, stop=False)
                    with pe.Fori(start, end) as c:
                        n = pe.snap(visit, min_val=0, max_val=NW * NCH)
                        pe.wait_ge(S["gen_ready"], n + 1)
                        mm(bank, gen_lo[:], gen_key[:], start=False, stop=False).then_inc(S["gen_free"], 1)
                        pe.reg_add(visit, visit, 1)
                    mm(psum[0:127, WIN, 0:MW], self_row[:, 128:255], self_cols[:], start=False, stop=True)\
                      .then_inc(S["gen_win"], 1)

            def window(w, j):
                free = {0: w, 1: w - 1}.get(j, w - 1)
                if free > 0:
                    pe.wait_ge(S["counts_ready"], free)
                pe.wait_ge(S["hot_ready"], w + 1)
                bank = psum[:, WIN + j % 2, 0:MW]
                mm(bank, self_row[:, 127 - w:255 - w], self_cols[:], start=True, stop=False)
                for k in range(KS):
                    ins = mm(bank, hot_lo[:, w % RING, :, k], hot_key[:, w % RING, k], start=False, stop=(k == KS - 1))
                ins.then_inc(S["win_done"], 1)

            def sums(g, part):
                if part == 0:
                    pe.wait_ge(S["counts_final"], g + 1)
                    if g >= 1:
                        pe.wait_ge(S["hT_ready"], 4 * g)
                for t in range(TP * part, TP * part + TP):
                    if g == 0:
                        pe.wait_ge(S["xn_hi_ready"], t + 1)
                        pe.wait_ge(S["xn_lo_ready"], t + 1)
                    for n, half in enumerate((xn_hi, xn_lo)):
                        for c in range(KC):
                            ins = mm(psum[:, AGG + c, 0:GN], half[:, t, c * 128:(c + 1) * 128], counts[0:P, g % 2, t],
                                     start=(t == 0 and n == 0), stop=(t == T - 1 and n == 1))
                if part == PARTS - 1:
                    ins.then_inc(S["agg_main"], 1)
                    with pe.If(flag > 0):
                        pe.wait_ge(S["rest_in"], 16 * (g + 1))
                        for t in range(T):
                            for half in (xn_hi, xn_lo):
                                for c in range(KC):
                                    mm(psum[:, AGG + c, 0:GN], half[:, t, c * 128:(c + 1) * 128], counts[0:P, g % 2, t],
                                       start=False, stop=(t == T - 1 and half is xn_lo), skip_group_check=True)
                    mm(psum[0:127, AGG + KC - 1, 0:MW], self_row[:, 128:255], self_cols[:], start=False, stop=True,
                       skip_group_check=True).then_inc(S["agg_done"], 1)

            def mlp1(g, m):
                if m == 0:
                    pe.wait_ge(S["hT_ready"], 4 * (g + 1))
                    pe.wait_ge(S["w_split"], 1)
                if m >= 2:
                    pe.wait_ge(S["relu_ready"], 4 * g + m - 1)
                elif g >= 1:
                    pe.wait_ge(S["x2_ready"], 4 * g + m - 1)
                cols = slice(m * 128, (m + 1) * 128)
                trio = [(W1_hi, hT_hi), (W1_lo, hT_hi), (W1_hi, hT_lo)]
                for k in range(KC):
                    for n, (w_, h_) in enumerate(trio):
                        ins = mm(psum[:, SM + m % 2, 0:GN], w_[:, k, cols], h_[:, k], start=(k == 0 and n == 0),
                                 stop=(k == KC - 1 and n == 2))
                ins.then_inc(S["mlp1_done"], 1)

            def mlp2(g, q):
                if q == 0:
                    pe.wait_ge(S["h1_split"], 4 * (g + 1))
                    pe.wait_ge(S["w_split"], 2)
                if q >= 2:
                    pe.wait_ge(S["x2_ready"], 4 * g + q - 1)
                elif g >= 1:
                    pe.wait_ge(S["gate_taken"], 4 * (g - 1) + q + 3)
                rows = slice(q * P, (q + 1) * P)
                trio = [(h1_hi, W2_hi), (h1_hi, W2_lo), (h1_lo, W2_hi)]
                for k in range(KC):
                    for n, (h_, w_) in enumerate(trio):
                        ins = mm(psum[0:P, SM + q % 2, :], h_[:, k, rows], w_[:, k], start=(k == 0 and n == 0),
                                 stop=(k == KC - 1 and n == 2))
                ins.then_inc(S["mlp2_done"], 1)

            def gate_turn(g, tiles):
                for q in tiles:
                    n = 4 * g + q
                    pe.wait_ge(S["xt_ready"], n + 1)
                    if q >= 2:
                        pe.wait_ge(S["gate_taken"], n - 1)
                    elif g + 1 < G:
                        pe.wait_ge(S["relu_ready"], 4 * (g + 1) + q + 3)
                    elif g + 1 == G:
                        pe.wait_ge(S["x2_ready"], 4 * G)
                    for c in range(KC):
                        ins = pe.transpose(psum[:, SM + q % 2, c * P:(c + 1) * P], xt[:, q, c * 128:(c + 1) * 128], ident[0:P, 0:P])
                    ins.then_inc(S["xt_turned"], 1)

            def gate(g, tiles):
                for q in tiles:
                    n = 4 * g + q
                    pe.wait_ge(S["xt_T_ready"], n + 1)
                    for c in range(KC):
                        ins = mm(psum[0:P, SM + q % 2, 0:NE], h1[:, q % 2, c * P:(c + 1) * P], Wg_sb[:, c],
                                 start=(c == 0), stop=(c == KC - 1))
                    ins.then_inc(S["gate_done"], 1)

            pe.wait_ge(S["small_in"], 48)
            for it in range(G + 3):
                for part in range(PARTS):
                    for j in range(WP):
                        if it < G:
                            window(WG * it + WP * part + j, j)
                        if 0 <= it - 3:
                            if (part, j) == (2, 2):
                                gate_turn(it - 3, (0, 1))
                            if (part, j) == (3, 0):
                                gate_turn(it - 3, (2, 3))
                            if (part, j) == (3, 3):
                                gate(it - 3, (2, 3))
                    if 0 <= it - 1 < G:
                        sums(it - 1, part)
                    if 0 <= it - 2 < G:
                        for m in mlp1_chunks(part):
                            mlp1(it - 2, m)
                        for q in mlp2_tiles(part):
                            mlp2(it - 2, q)
                    if 0 <= it - 3 and part == 2:
                        gate(it - 3, (0, 1))

            pe.wait_ge(S["chosen_ready"], 1)
            choices = either[:].rearrange("p n e -> p (n e)")
            mm(psum[0:P, 0, 0:T * NE], before[:], choices, start=True, stop=True)
            mm(psum[0:P, 1, 0:T * NE], ones16[:], choices, start=True, stop=True).then_inc(S["ranked"], 1)
            pe.wait_ge(S["spread_ready"], 1)
            for n in range(2 * T):
                ins = mm(psum[:, 2, 0:2 * NT], at_row[:, n], token_part[:, n].rearrange("p a s -> p (a s)"),
                         start=(n == 0), stop=(n == 2 * T - 1))
            ins.then_inc(S["spread_done"], 1)

            def turn(k):
                pe.wait_ge(S["x_now_ready"], k + 1)
                for i in range(2):
                    for c in range(KC):
                        ins = pe.transpose(psum[:, i, c * 128:(c + 1) * 128], x_now[:, i, c * 128:(c + 1) * 128], ident[:])
                    ins.then_inc(S["turned"], 1)

            turn(0)
            pe.wait_ge(S["tokens_ready"], 1)
            pe.wait_ge(S["slots_known"], 1)
            start = 0
            for e in range(NE):
                end = NB if e == NE - 1 else pe.value_load(end_i[0:1, e:e + 1], min_val=1, max_val=NB)
                pe.wait_ge(S["w_lo_ready"], e + 1)
                with pe.Fori(start, end) as k:
                    pe.wait_ge(S["xT_ready"], k * 2 + 2)
                    trio = [(w1_hi, xT_hi), (w1_lo, xT_hi), (w1_hi, xT_lo)]
                    for m in range(HC):
                        cols = slice(m * 128, (m + 1) * 128)
                        for c in range(KC):
                            for i, (w_, x_) in enumerate(trio):
                                ins = mm(psum[:, 2 + m, 0:B], w_[:, e, c, cols], x_[:, c], start=(c == 0 and i == 0),
                                         stop=(c == KC - 1 and i == 2))
                        ins.then_inc(S["up_done"], 1)
                    turn(k + 1)
                    trio = [(he_hi, w2_hi), (he_hi, w2_lo), (he_lo, w2_hi)]
                    for m in range(HC):
                        pe.wait_ge(S["he_ready"], k * 2 + (m + 1))
                        for i in range(2):
                            if m == 0:
                                pe.wait_ge((S["y0_taken"], S["y1_taken"])[i], k + 1)
                            for n, (h_, w_) in enumerate(trio):
                                ins = mm(psum[:, 4 + i, :], h_[:, m, i * 128:(i + 1) * 128], w_[:, e, m],
                                         start=(m == 0 and n == 0), stop=(m == HC - 1 and n == 2))
                            if m == HC - 1:
                                ins.then_inc(S["down_done"], 1)
                start = end

            pe.wait_ge(S["scores_ready"], 1)
            pe.wait_ge(S["eb_in"], 32)
            for n in range(T):
                if n % 4 == 0:
                    if n:
                        pe.wait_ge(S["scores_T_ready"], n // 4)
                    else:
                        pe.wait_ge(S["xT_ready"], 2 * (NB + 1))
                    for q in range(4):
                        ins = pe.transpose(psum[0:NE, 0, q * P:(q + 1) * P], scores[:, n + q], ident[0:P, 0:P])
                    ins.then_inc(S["scores_turned"], 1)
                    pe.wait_ge(S["scores_T_ready"], n // 4 + 1)
                if n >= 2:
                    pe.wait_ge(S["summed"], n - 1)
                mm(psum[0:P, 1 + n % 2, :], scores_T[:, n], eb2_sb[:], start=True, stop=True).then_inc(S["bias_done"], 1)


_INS = ["x", "src", "dst", "L0_gnn_W1", "L0_gnn_b1", "L0_gnn_W2", "L0_gnn_b2",
        "L0_ffn_Wg", "L0_ffn_W1", "L0_ffn_b1", "L0_ffn_W2", "L0_ffn_b2"]


def kernel(**inputs):
    import numpy as _np
    import concourse.bacc as _bacc
    from concourse.bass_utils import run_bass_kernel_spmd as _run

    nc = _bacc.Bacc("TRN2", target_bir_lowering=False, num_devices=1)
    arrays, args = {}, []
    for name in _INS:
        a = _np.ascontiguousarray(inputs[name])
        arrays[f"in_{name}"] = a
        args.append(nc.dram_tensor(f"in_{name}", a.shape, mybir.dt.from_np(a.dtype), kind="ExternalInput").ap())
    args.append(nc.dram_tensor("out_x", (N, D), F32, kind="ExternalOutput").ap())
    gnn_moe(nc, *args)
    r = _run(nc, [arrays], core_ids=[0])
    return r.results[0]["out_x"]
```

```python
from contextlib import ExitStack

import concourse.bass as bass
from concourse import mybir

F32 = mybir.dt.float32
F32R = mybir.dt.float32r
F16 = mybir.dt.float16
BF16 = mybir.dt.bfloat16
I32 = mybir.dt.int32
U32 = mybir.dt.uint32
ALU = mybir.AluOpType
ACT = mybir.ActivationFunctionType
AX = mybir.AxisListType

N, D, E = 2500, 512, 80000
P = 125
T = N // P
KC = D // 128
CH = 128
NCH = E // CH
CPP = NCH // P
W = 20
NW = N // W
MW = W * T
HW = W // 2
MH = MW // 2
KS = 4
SL = 2 * KS
FULL = 255
ROWS = 640
G = 5
GN = N // G
WG = NW // G
PARTS = 5
WP = WG // PARTS
TP = T // PARTS
LOOK = 3
RING = 4
NE, H, HC = 8, 256, 2
B = 256
NB = (2 * N + NE * (B - 1)) // B
MOST = -(-N // B)
SPREAD = 8
NT = 2 * (NB + 1)
FAR = -1.0e4
EPS = 1e-5
ROUND = 12582912.0


def gnn_moe(nc, x, src, dst, gW1, gb1, gW2, gb2, Wg, eW1, eb1, eW2, eb2, out):
    ctx = ExitStack()
    with ctx:
        def sem(name):
            return ctx.enter_context(nc.semaphore(name))

        def allocator(stack):
            return lambda name, shape, dt: stack.enter_context(nc.sbuf_tensor(name, shape, dt))

        edge_rows = nc.dram_tensor("edge_rows", [ROWS, 2 * CH], F32).ap()
        spans_d = nc.dram_tensor("spans_d", [2, NCH], F32).ap()
        x2_d = nc.dram_tensor("x2_d", [N, D], F32).ap()
        xt_d = nc.dram_tensor("xt_d", [N, D], F32).ap()
        y_d = nc.dram_tensor("y_d", [NB * B, D], F32).ap()
        range_d = nc.dram_tensor("range_d", [1, 2 * NW + 1], I32).ap()
        counts_d = nc.dram_tensor("counts_d", [2, 128, T, N], BF16).ap()

        keep = allocator(ctx)
        eps_t = keep("eps_t", [128, 1], F32)
        ident = keep("ident", [128, 128], F32)
        ones = keep("ones", [P, 1], F32)
        flag_i = keep("flag_i", [1, 1], I32)
        range_row = keep("range_row", [1, 2 * NW + 1], I32)
        iota_e = keep("iota_e", [P, NE], F32)
        Wg_sb = keep("Wg_sb", [128, KC, NE], F32)
        logits = keep("logits", [P, T, NE], F32)
        top = keep("top", [P, T, 8], F32)
        topi = keep("topi", [P, T, 8], U32)

        graph = ExitStack()
        sb = allocator(graph)
        xn_hi = sb("xn_hi", [P, T, D], F16)
        xn_lo = sb("xn_lo", [P, T, D], F16)
        general = ExitStack()
        gb = allocator(general)
        key_all = gb("key_all", [128, ROWS], F32)
        lo_all = gb("lo_all", [128, ROWS], F32)
        gen_iota = gb("gen_iota", [128, MW], F16)
        gen_key = gb("gen_key", [128, MW], F16)
        gen_lo = gb("gen_lo", [128, 128], F16)
        gen_counts = gb("gen_counts", [128, 2, T, W], BF16)
        general.close()
        counts = sb("counts", [128, 2, T, GN], BF16)
        gather = ExitStack()
        slot_rows = allocator(gather)("slot_rows", [NW, SL, 2 * CH], F32)
        dst_next = allocator(gather)("dst_next", [P, 2, CPP * CH], I32)
        gather.close()
        hot_key = sb("hot_key", [128, RING, 2, MH, KS], F16)
        hot_lo = sb("hot_lo", [128, RING, 2, 128, KS], F16)
        W1_hi, W1_lo, W2_hi, W2_lo = (sb(n, [128, KC, D], F32R) for n in ("W1_hi", "W1_lo", "W2_hi", "W2_lo"))
        b1_col = sb("b1_col", [128, KC], F32)
        b2_row = sb("b2_row", [P, D], F32)
        key_w = sb("key_w", [128, NW, SL], F16)
        lo_w = sb("lo_w", [128, NW, SL], F16)
        iota_key = sb("iota_key", [128, MH, KS], F16)
        iota_lo = sb("iota_lo", [128, 128, KS], F16)
        win_base = sb("win_base", [128, 2, NW], F32)
        self_row = sb("self_row", [128, 255], F16)
        self_cols = sb("self_cols", [128, MW], F16)

        early = ExitStack()
        sb = allocator(early)
        x_in = sb("x_in", [P, 4, D], F32)
        xn = sb("xn", [P, 2, D], F32)
        stat1 = sb("stat1", [P, T, 6], F32)
        mv1 = sb("mv1", [P, T, 2], F32)
        std1 = sb("std1", [P, T], F32)
        rstd1 = sb("rstd1", [P, T], F32)
        W_raw = sb("W_raw", [128, KC, D], F32)
        dst_i = sb("dst_i", [P, CPP * CH], I32)
        src_i = sb("src_i", [P, CPP * CH], I32)
        edge_a = sb("edge_a", [P, CPP, CH], F32)
        edge_rows_sb = sb("edge_rows_sb", [P, CPP, 2, CH], F32)
        pad_rows = sb("pad_rows", [ROWS - NCH, 2 * CH], F32)
        spans = sb("spans", [P, 2, CPP], F32)
        spans_b = sb("spans_b", [NW, 2, NCH], F32)
        hit = sb("hit", [NW, 2, NCH], F32)
        chunk_up = sb("chunk_up", [NW, NCH], F32)
        chunk_down = sb("chunk_down", [NW, NCH], F32)
        win_lo = sb("win_lo", [NW, 2], F32)
        win_hi = sb("win_hi", [NW, 2], F32)
        first, last = (sb(n, [NW, 2], F32) for n in ("first", "last"))
        whole = sb("whole", [NW, 2], F32)
        span_i = sb("span_i", [NW, 2], I32)
        flaw = sb("flaw", [P, 5], F32)
        slot_iota = sb("slot_iota", [NW, KS], F32)
        slot_i = sb("slot_i", [NW, 2, KS], I32)
        early.close()

        late = ExitStack()
        sb = allocator(late)
        hT_hi = sb("hT_hi", [128, KC, GN], F32R)
        hT_lo = sb("hT_lo", [128, KC, GN], F32R)
        h1 = sb("h1", [128, 2, GN], F32)
        h1_hi = sb("h1_hi", [128, KC, GN], F32R)
        h1_lo = sb("h1_lo", [128, KC, GN], F32R)
        x_res = sb("x_res", [P, 2, D], F32)
        x2 = sb("x2", [P, 2, D], F32)
        xt = sb("xt", [P, 4, D], F32)
        ln2 = sb("ln2", [P, 2, 10], F32)
        late.close()
        graph.close()

        ffn = ExitStack()
        sb = allocator(ffn)
        back = ExitStack()
        x2_back = allocator(back)("x2_back", [P, T, D], F32)
        back.close()
        w_raw = sb("w_raw", [128, 2, 2, KC * H], F32)
        w1_hi, w1_lo, w2_hi, w2_lo = [], [], [], []
        for e in range(NE):
            for name, tensors, shape in (("w1_hi", w1_hi, [128, KC, H]), ("w1_lo", w1_lo, [128, KC, H]),
                                         ("w2_hi", w2_hi, [128, HC, D]), ("w2_lo", w2_lo, [128, HC, D])):
                tensors.append(sb(f"{name}_{e}", shape, F32R))
        eb1_col = sb("eb1_col", [128, NE * HC], F32)
        eb2_sb = sb("eb2_sb", [NE, D], F32)
        dest_i = sb("dest_i", [P, 2 * T], I32)
        token_i = sb("token_i", [128, NT], I32)
        expert_i = sb("expert_i", [1, NB], I32)
        end_i = sb("end_i", [1, NE], I32)
        chosen = sb("chosen", [P, 2, T, NE], F32)
        shifted = sb("shifted", [P, T, NE], F32)
        total = sb("total", [P, T], F32)
        share = sb("share", [P, 2, T], F32)
        share_sum = sb("share_sum", [P, T], F32)
        scores = sb("scores", [P, T, NE], F32)
        scores_T = sb("scores_T", [NE, T, P], F32)

        route = ExitStack()
        sb = allocator(route)
        before = sb("before", [P, P], F16)
        ones16 = sb("ones16", [P, P], F16)
        topf = sb("topf", [P, 2, T], F32)
        either = sb("either", [P, T, NE], F16)
        goes_on = sb("goes_on", [P, NE, T], F32)
        tile_count = sb("tile_count", [P, NE, T], F32)
        count_up = sb("count_up", [P, NE, T], F32)
        slot_of = sb("slot_of", [P, NE, T], F32)
        blocks = sb("blocks", [P, NE], F32)
        block_end = sb("block_end", [P, NE], F32)
        block_base = sb("block_base", [P, NE], F32)
        picked = sb("picked", [P, 2, T, NE], F32)
        dest = sb("dest", [P, 2 * T], F32)
        dest_tile = sb("dest_tile", [P, 2 * T], F32)
        dest_tile16 = sb("dest_tile16", [P, 2 * T], F16)
        dest_row = sb("dest_row", [P, 2 * T], F16)
        iota_128 = sb("iota_128", [P, 128], F16)
        iota_nt = sb("iota_nt", [P, NT], F16)
        iota_n = sb("iota_n", [P, 2, T], F16)
        iota_p = sb("iota_p", [P, 1], F32)
        iota_k = sb("iota_k", [1, NB], F32)
        at_row = sb("at_row", [P, 2 * T, 128], F16)
        at_tile = sb("at_tile", [P, 2 * T, NT], F16)
        token_part = sb("token_part", [P, 2 * T, 2, NT], F16)
        token_low = sb("token_low", [128, NT], F32)
        ends_before = sb("ends_before", [1, NB, NE], F32)
        expert_f = sb("expert_f", [1, NB], F32)
        route.close()

        work = ExitStack()
        sb = allocator(work)
        xg = sb("xg", [128, 2, 2, D], F32)
        x_now = sb("x_now", [128, 2, D], F32)
        xT_hi, xT_lo = (sb(n, [128, KC, B], F32R) for n in ("xT_hi", "xT_lo"))
        he = sb("he", [128, HC, B], F32)
        he_hi, he_lo = (sb(n, [128, HC, B], F32R) for n in ("he_hi", "he_lo"))
        y = sb("y", [128, 2, 2, D], F32)
        work.close()

        join = ExitStack()
        sb = allocator(join)
        y_back = sb("y_back", [P, 4, 2, D], F32)
        join.close()
        ffn.close()

        psum = ctx.enter_context(nc.psum_tensor("psum", [128, 8, 512], F32))
        WIN, AGG, SM = 0, 2, 6

        names = (
            "dst_in src_in next_blank next_in x_in_a x_in_b x_in_c x_in_d w1_in w2_in small_in tables spans_ready keys_ready "
            "spans_out spans_in rows_out idx_ready gathered rows_turned rows_used stats_ready std_ready xn_ready xn_hi_ready "
            "xn_lo_ready w_split flaws_ready flaws_done range_ready range_out range_in bounds_step bounds_ready bounds_out bounds_in "
            "gen_cleared gen_turned gen_taken gen_free gen_ready gen_win gen_half gen_split gen_stored gen_saved counts_in rest_in "
            "hot_ready win_done counts_ready counts_final agg_main agg_done hT_hi_ready hT_ready mlp1_done relu_ready h1_split "
            "mlp2_done x2_ready std2_ready xt_ready res_in_a res_in_b res_sum x2_out_a x2_out_b xt_turned xt_T_ready gate_done "
            "gate_taken top_ready topi_ready dve_step act_step pool_step "
            "x2_landed route_tables chosen_ready ranked slots_known at_tile_ready parts_ready spread_ready spread_done tokens_ready shifted_ready exp_ready "
            "scores_ready scores_turned scores_T_ready "
            "ew_in_a ew_in_b w_hi_ready w_lo_ready eb_in xg_in_a xg_in_b x_now_ready turned xT_hi_ready xT_ready up_done "
            "gelu_ready he_ready down_done y0_taken y1_taken y_out_a y_out_b yb_in_a yb_in_b yb_in_c yb_in_d "
            "x2_back_in bias_done bias_added summed out_a out_b out_c out_d").split()
        S = {n: sem(n) for n in names}

        block = ctx.enter_context(nc.Block())
        x_tiles = x.rearrange("(p t) d -> p t d", t=T)
        x_in_sems = [S["x_in_a"], S["x_in_b"], S["x_in_c"], S["x_in_d"]]
        res_in = [S["res_in_a"], S["res_in_b"]]
        x2_out = [S["x2_out_a"], S["x2_out_b"]]
        ew_in = [S["ew_in_a"], S["ew_in_b"]]
        xg_in = [S["xg_in_a"], S["xg_in_b"]]
        y_out = [S["y_out_a"], S["y_out_b"]]
        yb_in = [S["yb_in_" + c] for c in "abcd"]
        out_done = [S["out_" + c] for c in "abcd"]

        def stepper(eng, s):
            count = [0]

            def step(ins):
                ins.then_inc(s, 1)
                count[0] += 1
                eng.wait_ge(s, count[0])
            return step

        def mlp1_chunks(part):
            return {0: (0, 1), 1: (2, 3)}.get(part, ())

        def mlp2_tiles(part):
            return {3: (0, 1), 4: (2, 3)}.get(part, ())

        @block.sync
        def _(sp):
            sp.dma_start(dst_i[:], dst.rearrange("(p e) -> p e", p=P)).then_inc(S["dst_in"], 16)
            sp.dma_start(src_i[:], src.rearrange("(p e) -> p e", p=P)).then_inc(S["src_in"], 16)
            sp.wait_ge(S["next_blank"], 1)
            row = CPP * CH
            for n, ahead in enumerate((1, FULL)):
                sp.dma_start(dst_next[0:P - 1, n], dst[ahead:ahead + (P - 1) * row].rearrange("(p e) -> p e", e=row))\
                  .then_inc(S["next_in"], 16)
                sp.dma_start(dst_next[P - 1:P, n, 0:row - ahead], dst[ahead + (P - 1) * row:E].rearrange("(o e) -> o e", o=1))\
                  .then_inc(S["next_in"], 16)
            for t in range(T):
                if t == 4:
                    sp.wait_ge(S["spans_ready"], 1)
                    sp.dma_start(spans_d.rearrange("a (p c) -> p a c", p=P), spans[:]).then_inc(S["spans_out"], 16)
                    sp.wait_ge(S["tables"], 1)
                    sp.dma_start(edge_rows[NCH:ROWS, :], pad_rows[:]).then_inc(S["rows_out"], 16)
                    sp.wait_ge(S["keys_ready"], 1)
                    sp.dma_start(edge_rows[0:NCH, :].rearrange("(p c) e -> p (c e)", p=P),
                                 edge_rows_sb[:].rearrange("p c a e -> p (c a e)")).then_inc(S["rows_out"], 16)
                    sp.wait_ge(S["spans_out"], 16)
                    sp.dma_start(spans_b[:], spans_d.rearrange("(o a) c -> o a c", o=1).broadcast_to([NW, 2, NCH])).then_inc(S["spans_in"], 16)
                if t >= 4:
                    sp.wait_ge(S["xn_ready"], t - 3)
                sp.dma_start(x_in[:, t % 4], x_tiles[:, t]).then_inc(x_in_sems[t % 4], 16)
            sp.wait_ge(S["range_ready"], 2)
            sp.dma_start(range_d[:, 2 * NW:], flag_i[:]).then_inc(S["range_out"], 16)
            sp.wait_ge(S["range_out"], 16)
            sp.dma_start(range_row[:, 2 * NW:], range_d[:, 2 * NW:]).then_inc(S["range_in"], 16)
            sp.wait_ge(S["range_in"], 16)
            flag = sp.value_load(range_row[0:1, 2 * NW:], min_val=0, max_val=1)

            with sp.If(flag > 0):
                sp.wait_ge(S["bounds_ready"], 1)
                sp.dma_start(range_d[0, 0:2 * NW].rearrange("(w a) -> w a", a=2), span_i[:]).then_inc(S["bounds_out"], 16)
                sp.wait_ge(S["bounds_out"], 16)
                sp.dma_start(range_row[:, 0:2 * NW], range_d[:, 0:2 * NW]).then_inc(S["bounds_in"], 16)
                sp.wait_ge(S["bounds_in"], 16)
                sp.sem_inc(S["gen_stored"], 1)
                with sp.Fori(0, NW) as w:
                    sp.wait_ge(S["gen_split"], w + 1)
                    for n in range(2):
                        sp.dma_start(counts_d[n, :, :, bass.ds(w * W, W)], gen_counts[:, n]).then_inc(S["gen_saved"], 16)
                    sp.wait_ge(S["gen_saved"], (w + 1) * 32)
                    sp.sem_inc(S["gen_stored"], 1)

            def store(g, tiles):
                for q in tiles:
                    n = 4 * g + q
                    rows = slice(n * P, (n + 1) * P)
                    sp.wait_ge(S["xt_ready"], n + 1)
                    sp.dma_start(x2_d[rows, :], x2[:, q % 2]).then_inc(x2_out[q % 2], 16)
                    sp.dma_start(xt_d[rows, :], xt[:, q]).then_inc(x2_out[q % 2], 16)

            def group_counts(n, g):
                return counts[:, g % 2], counts_d[n, :, :, g * GN:(g + 1) * GN]

            def load_expert(e):
                if e >= 2:
                    sp.wait_ge(S["w_hi_ready"], e - 1)
                    sp.wait_ge(S["w_lo_ready"], e - 1)
                sp.dma_start(w_raw[:, e % 2, 0].rearrange("p (k h) -> p k h", k=KC),
                             eW1[e].rearrange("(k p) h -> p k h", p=128)).then_inc(ew_in[e % 2], 16)
                sp.dma_start(w_raw[:, e % 2, 1].rearrange("p (k h) -> p k h", k=HC),
                             eW2[e].rearrange("(k p) h -> p k h", p=128)).then_inc(ew_in[e % 2], 16)

            for it in range(G + 3):
                if 0 <= it - 3:
                    store(it - 3, (2, 3))
                if it == G + 1:
                    sp.wait_ge(S["agg_done"], G)
                    load_expert(0)
                    load_expert(1)
                if 0 <= it - 2 < G:
                    store(it - 2, (0, 1))
                if it == G + 1:
                    load_expert(2)
                if 0 <= it - 1 < G:
                    with sp.If(flag > 0):
                        sp.wait_ge(S["agg_main"], it)
                        sp.dma_start(*group_counts(1, it - 1)).then_inc(S["rest_in"], 16)
                if it < G:
                    sp.wait_ge(S["counts_ready"], WG * (it + 1))
                    with sp.If(flag > 0):
                        sp.dma_start(*group_counts(0, it)).then_inc(S["counts_in"], 16)
                        sp.wait_ge(S["counts_in"], 16 * (it + 1))
                    sp.sem_inc(S["counts_final"], 1)
            for b in range(2):
                sp.wait_ge(x2_out[b], 32 * 2 * G)
            sp.sem_inc(S["x2_landed"], 1)
            for e in range(3, NE):
                if e == 4:
                    sp.wait_ge(S["gate_done"], T)
                    sp.dma_start(eb1_col[:], eb1.rearrange("e (k p) -> p (e k)", p=128), allow_slow_non_contiguous=True).then_inc(S["eb_in"], 16)
                    sp.dma_start(eb2_sb[:], eb2[:, :]).then_inc(S["eb_in"], 16)
                load_expert(e)
            for k in range(NB):
                if k in (MOST + 1, 2 * MOST + 1):
                    sp.wait_ge(S["w_hi_ready"], NE)
                    sp.wait_ge(S["w_lo_ready"], NE)
                    for n in range(16 * (k // (2 * MOST)), (16, T)[k // (2 * MOST)], 4):
                        sp.dma_start(x2_back[:, n:n + 4], x2_d[n * P:(n + 4) * P, :].rearrange("(n p) d -> p n d", p=P))\
                          .then_inc(S["x2_back_in"], 16)
                sp.wait_ge(S["y0_taken"], k + 2)
                sp.wait_ge(S["y1_taken"], k + 2)
                sp.dma_start(y_d[k * B:(k + 1) * B, :].rearrange("(i p) d -> p i d", p=128), y[:, k % 2]).then_inc(y_out[k % 2], 16)
            for n in range(T):
                sp.wait_ge(S["summed"], n + 1)
                sp.dma_start(out[n * P:(n + 1) * P, :], x2_back[:, n]).then_inc(out_done[n % 4], 16)
            for b in range(4):
                sp.wait_ge(out_done[b], 16 * (T // 4))

        @block.gpsimd
        def _(pool):
            step = stepper(pool, S["pool_step"])
            small = dict(allow_small_or_imprecise_dtypes=True)
            pool.memset(dst_next[:, 0], N)
            pool.memset(dst_next[:, 1], -1).then_inc(S["next_blank"], 1)
            pool.memset(ones[:], 1.0)
            pool.iota(chunk_up[:], pattern=[[1, NCH]], base=1, channel_multiplier=0, **small)
            pool.iota(chunk_down[:], pattern=[[-1, NCH]], base=NCH, channel_multiplier=0, **small)
            pool.iota(win_lo[:], pattern=[[HW, 2]], base=0, channel_multiplier=W, **small)
            pool.iota(win_hi[:], pattern=[[HW, 2]], base=HW - 1, channel_multiplier=W, **small)
            pool.iota(slot_iota[:], pattern=[[1, KS]], base=0, channel_multiplier=0, **small)
            pool.memset(pad_rows[:, 0:CH], FAR)
            pool.memset(pad_rows[:, CH:2 * CH], -1.0).then_inc(S["tables"], 1)
            pool.memset(ident[:], 0.0)
            pool.memset(eps_t[:], EPS)
            pool.iota(iota_e[:], pattern=[[1, NE]], base=0, channel_multiplier=0, **small)
            pool.memset(lo_w[:], -1.0)
            pool.memset(self_row[:], 0.0)
            step(pool.memset(self_cols[:], 0.0))
            pool.affine_select(out=ident[:], in_=ident[:], compare_op=ALU.not_equal, fill=1.0, base=0,
                               pattern=[[-1, 128]], channel_multiplier=1)
            pool.affine_select(out=self_row[:], in_=self_row[:], compare_op=ALU.not_equal, fill=1.0, base=127,
                               pattern=[[-1, 255]], channel_multiplier=1000)
            cols = self_cols[:].rearrange("p (w h) -> p w h", w=W)
            pool.affine_select(out=cols, in_=cols, compare_op=ALU.not_equal, fill=1.0, base=0,
                               pattern=[[1, W], [-1, T]], channel_multiplier=0)
            pool.iota(gen_iota[:], pattern=[[1, MW]], base=0, channel_multiplier=0, **small)
            pool.iota(iota_key[:], pattern=[[1, MH], [0, KS]], base=0, channel_multiplier=0, **small)
            pool.iota(iota_lo[:], pattern=[[1, 128], [0, KS]], base=0, channel_multiplier=0, **small)
            pool.iota(win_base[:], pattern=[[MH, 2], [MW, NW]], base=0, channel_multiplier=0, **small).then_inc(S["tables"], 1)

            def low_parts(a, b):
                for t in range(a, b):
                    pool.wait_ge(S["xn_hi_ready"], t + 1)
                    pool.tensor_tensor(xn_lo[:, t], xn[:, t % 2], xn_hi[:, t], ALU.subtract).then_inc(S["xn_lo_ready"], 1)

            low_parts(0, LOOK)
            pool.wait_ge(S["idx_ready"], 1)
            pool.wait_ge(S["rows_out"], 32)
            for k in range(SL):
                pool.indirect_dma_start(out=slot_rows[:, k], out_offset=None, in_=edge_rows[:, :],
                                        in_offset=bass.IndirectOffsetOnAxis(ap=slot_i[:, k // KS, k % KS:k % KS + 1], axis=0),
                                        bounds_check=ROWS - 1).then_inc(S["gathered"], 16)
            low_parts(LOOK, T)
            for n, (hi, lo, s) in enumerate(((W1_hi, W1_lo, S["w1_in"]), (W2_hi, W2_lo, S["w2_in"]))):
                pool.wait_ge(s, 16)
                step(pool.tensor_copy(hi[:], W_raw[:]))
                pool.tensor_tensor(lo[:], W_raw[:], hi[:].bitcast(F32), ALU.subtract).then_inc(S["w_split"], 1)

            def split_low(e):
                pool.wait_ge(ew_in[e % 2], 32 * (e // 2 + 1))
                pool.wait_ge(S["w_hi_ready"], e + 1)
                pool.tensor_tensor(w1_lo[e][:], w_raw[:, e % 2, 0].rearrange("p (k h) -> p k h", k=KC), w1_hi[e][:].bitcast(F32), ALU.subtract)
                pool.tensor_tensor(w2_lo[e][:], w_raw[:, e % 2, 1].rearrange("p (k h) -> p k h", k=HC), w2_hi[e][:].bitcast(F32), ALU.subtract)\
                    .then_inc(S["w_lo_ready"], 1)

            pool.wait_ge(S["small_in"], 48)
            for g in range(G):
                for m in range(KC):
                    pool.wait_ge(S["relu_ready"], 4 * g + m + 1)
                    if m == 0 and g >= 1:
                        pool.wait_ge(S["mlp2_done"], 4 * g)
                    pool.tensor_tensor(h1_lo[:, m], h1[:, m % 2], h1_hi[:, m].bitcast(F32), ALU.subtract)\
                        .then_inc(S["h1_split"], 1)
                for q in range(4):
                    pool.wait_ge(res_in[q % 2], 16 * (2 * g + q // 2 + 1))
                    pool.tensor_tensor(x_res[:, q % 2], x_res[:, q % 2], b2_row[:], ALU.add).then_inc(S["res_sum"], 1)
                    if g == G - 1 and q == 1:
                        split_low(0)
            for e in range(1, 3):
                split_low(e)

            pool.wait_ge(S["x2_landed"], 1)
            pool.wait_ge(S["gate_done"], T)
            pool.iota(iota_128[:], pattern=[[1, 128]], base=0, channel_multiplier=0, **small)
            pool.iota(iota_nt[:], pattern=[[1, NT]], base=0, channel_multiplier=0, **small)
            pool.iota(iota_n[:], pattern=[[0, 2], [1, T]], base=0, channel_multiplier=0, **small)
            pool.iota(iota_p[:], pattern=[[0, 1]], base=0, channel_multiplier=1, **small)
            pool.iota(iota_k[:], pattern=[[1, NB]], base=0, channel_multiplier=0, **small)
            pool.memset(ones16[:], 1.0)
            pool.memset(before[:], 1.0)
            step(pool.memset(goes_on[:], 1.0))
            pool.affine_select(out=before[:], in_=before[:], compare_op=ALU.is_gt, fill=0.0, base=0,
                               pattern=[[1, P]], channel_multiplier=-1)
            pool.affine_select(out=goes_on[:], in_=goes_on[:], compare_op=ALU.is_gt, fill=0.0, base=0,
                               pattern=[[0, NE], [1, T]], channel_multiplier=0).then_inc(S["route_tables"], 1)

            def gather(k):
                if k >= 2:
                    pool.wait_ge(S["x_now_ready"], k - 1)
                for i in range(2):
                    pool.indirect_dma_start(out=xg[:, k % 2, i], out_offset=None, in_=xt_d[:, :],
                                            in_offset=bass.IndirectOffsetOnAxis(ap=token_i[:, 2 * k + i:2 * k + i + 1], axis=0),
                                            bounds_check=N - 1).then_inc(xg_in[k % 2], 16)

            for e in range(3, NE - 2):
                split_low(e)
            pool.wait_ge(S["tokens_ready"], 1)
            for k in range(NB + 1):
                gather(k)
                if k in (3, 5):
                    split_low(NE - 2 + (k - 3) // 2)
            for b in range(2):
                pool.wait_ge(y_out[b], 16 * ((NB + 1 - b) // 2))
            for n in range(T):
                if n >= 4:
                    pool.wait_ge(S["summed"], n - 3)
                for c in range(2):
                    pool.indirect_dma_start(out=y_back[:, n % 4, c], out_offset=None, in_=y_d[:, :],
                                            in_offset=bass.IndirectOffsetOnAxis(ap=dest_i[:, c * T + n:c * T + n + 1], axis=0),
                                            bounds_check=NB * B - 1).then_inc(yb_in[n % 4], 16)

        @block.scalar
        def _(act):
            step = stepper(act, S["act_step"])
            for n, (raw, s) in enumerate(((gW1, S["w1_in"]), (gW2, S["w2_in"]))):
                if n:
                    act.wait_ge(S["w_split"], 1)
                act.dma_start(W_raw[:], raw.rearrange("(k p) n -> p k n", p=128)).then_inc(s, 16)
                if n == 0:
                    act.dma_start(Wg_sb[:], Wg.rearrange("(k p) e -> p k e", p=128)).then_inc(S["small_in"], 16)
                    act.dma_start(b1_col[:], gb1.rearrange("(k p) -> p k", p=128), allow_slow_non_contiguous=True).then_inc(S["small_in"], 16)
                    act.dma_start(b2_row[:], gb2.rearrange("(o n) -> o n", o=1).broadcast_to([P, D])).then_inc(S["small_in"], 16)
                    act.wait_ge(S["tables"], 2)
                    for t in range(T):
                        act.wait_ge(S["stats_ready"], t + 1)
                        act.activation(std1[:, t:t + 1], mv1[:, t, 1:2], ACT.Sqrt, bias=eps_t[0:P, 0:1]).then_inc(S["std_ready"], 1)
                        if t >= 1:
                            act.wait_ge(S["xn_ready"], t)
                            act.activation(xn_hi[:, t - 1], xn[:, (t - 1) % 2], ACT.Copy).then_inc(S["xn_hi_ready"], 1)
                    act.wait_ge(S["xn_ready"], T)
                    act.activation(xn_hi[:, T - 1], xn[:, (T - 1) % 2], ACT.Copy).then_inc(S["xn_hi_ready"], 1)

            act.wait_ge(S["small_in"], 48)

            def load_residual(g, q):
                n = 4 * g + q
                if n >= 2:
                    act.wait_ge(S["x2_ready"], n - 1)
                act.dma_start(x_res[:, q % 2], x[n * P:(n + 1) * P, :]).then_inc(res_in[q % 2], 16)

            def std2s(g, tiles):
                for q in tiles:
                    act.wait_ge(S["x2_ready"], 4 * g + q + 1)
                    act.activation(ln2[:, q % 2, 8:9], ln2[:, q % 2, 7:8], ACT.Sqrt, bias=eps_t[0:P, 0:1])\
                       .then_inc(S["std2_ready"], 1)
                    if q < 2:
                        load_residual(g, q + 2)

            def gate_rows(g, tiles):
                for q in tiles:
                    n = 4 * g + q
                    act.wait_ge(S["xt_turned"], n + 1)
                    if q == 0 and g + 1 < G:
                        act.wait_ge(S["h1_split"], 4 * (g + 2))
                    if q >= 2:
                        act.wait_ge(S["gate_done"], n - 1)
                    act.activation(h1[:, q % 2], psum[:, SM + q % 2, 0:KC * P], ACT.Copy).then_inc(S["xt_T_ready"], 1)

            def split_high(e):
                act.wait_ge(ew_in[e % 2], 32 * (e // 2 + 1))
                act.activation(w1_hi[e][:], w_raw[:, e % 2, 0].rearrange("p (k h) -> p k h", k=KC), ACT.Copy)
                act.activation(w2_hi[e][:], w_raw[:, e % 2, 1].rearrange("p (k h) -> p k h", k=HC), ACT.Copy).then_inc(S["w_hi_ready"], 1)

            for it in range(G + 3):
                g = it - 2
                for part in range(PARTS):
                    if 0 <= g < G and part == 0:
                        if g == 0:
                            act.wait_ge(S["w_split"], 2)
                        act.wait_ge(S["agg_done"], g + 1)
                        for c in range(KC):
                            if c == 0 and g >= 1:
                                act.wait_ge(S["mlp1_done"], 4 * g)
                            act.activation(hT_hi[:, c], psum[:, AGG + c, 0:GN], ACT.Copy).then_inc(S["hT_hi_ready"], 1)
                    if part == 0 and 0 <= g - 1 < G:
                        std2s(g - 1, (2, 3))
                        if g == G:
                            split_high(2)
                    if g == G - 1 and part in (2, 3):
                        split_high(part - 2)
                    if part == 4 and 0 <= g < G:
                        std2s(g, (0, 1))
                    for j in range(WP):
                        if it < G:
                            w = WG * it + WP * part + j
                            act.wait_ge(S["win_done"], w + 1)
                            if part == 0 and j == 0 and it >= 2:
                                act.wait_ge(S["agg_done"], it - 1)
                            place = W * (WP * part + j)
                            act.activation(counts[:, it % 2, :, place:place + W],
                                           psum[:, WIN + j % 2, 0:MW].rearrange("p (w h) -> p h w", w=W),
                                           ACT.Copy).then_inc(S["counts_ready"], 1)
                        if 0 <= it - 3 and (part, j) == (2, 2):
                            gate_rows(it - 3, (0, 1))
                        if 0 <= it - 3 and (part, j) == (3, 0):
                            gate_rows(it - 3, (2, 3))
                    if 0 <= g < G:
                        for m in mlp1_chunks(part):
                            act.wait_ge(S["mlp1_done"], 4 * g + m + 1)
                            if 4 * g + m >= 2:
                                act.wait_ge(S["h1_split"], 4 * g + m - 1)
                            if m < 2 and g >= 2:
                                act.wait_ge(S["gate_done"], 4 * (g - 1))
                            if m == 0 and g >= 1:
                                act.wait_ge(S["mlp2_done"], 4 * g)
                            for half in (h1[:, m % 2], h1_hi[:, m]):
                                ins = act.activation(half, psum[:, SM + m % 2, 0:GN], ACT.Relu, bias=b1_col[:, m:m + 1])
                            ins.then_inc(S["relu_ready"], 1)
                        if part == 2:
                            load_residual(g, 0)
                            load_residual(g, 1)

            act.wait_ge(S["x2_landed"], 1)
            split_high(3)
            act.wait_ge(S["shifted_ready"], 1)
            act.activation(shifted[:], shifted[:], ACT.Exp)
            act.activation(share[:], share[:], ACT.Exp).then_inc(S["exp_ready"], 1)
            split_high(4)
            act.wait_ge(S["at_tile_ready"], 1)
            act.activation(token_part[:, :, 0], at_tile[:], ACT.Copy, scale=iota_p[:]).then_inc(S["parts_ready"], 1)
            split_high(5)
            split_high(6)

            def take_block(k):
                act.wait_ge(xg_in[k % 2], 32 * (k // 2 + 1))
                if k >= 1:
                    act.wait_ge(S["turned"], 2 * k)
                act.activation(x_now[:], xg[:, k % 2], ACT.Copy).then_inc(S["x_now_ready"], 1)

            def turned_high(k):
                for i in range(2):
                    act.wait_ge(S["turned"], 2 * k + i + 1)
                    act.activation(xT_hi[:, :, i * 128:(i + 1) * 128], psum[:, i].rearrange("p (c n) -> p c n", c=KC), ACT.Copy)\
                       .then_inc(S["xT_hi_ready"], 1)

            take_block(0)
            turned_high(0)
            take_block(1)
            split_high(7)
            act.wait_ge(S["eb_in"], 32)
            act.wait_ge(S["slots_known"], 1)
            act.sem_inc(S["y1_taken"], 1)
            for k in range(NB):
                expert = act.value_load(expert_i[0:1, k:k + 1], min_val=0, max_val=NE - 1)
                for m in range(HC):
                    act.wait_ge(S["up_done"], HC * k + m + 1)
                    if k >= 1:
                        act.wait_ge(S["he_ready"], HC * (k - 1) + m + 1)
                    act.activation(he[:, m], psum[:, 2 + m, 0:B], ACT.Gelu, bias=eb1_col[:, bass.ds(expert * HC + m, 1)])\
                       .then_inc(S["gelu_ready"], 1)
                turned_high(k + 1)
                if k + 2 <= NB:
                    take_block(k + 2)
                act.wait_ge(S["down_done"], 2 * k + 2)
                if k >= 2:
                    act.wait_ge(y_out[k % 2], 16 * (k // 2))
                act.activation(y[:, k % 2, 1], psum[:, 5], ACT.Copy).then_inc(S["y1_taken"], 1)

        @block.vector
        def _(dve):
            step = stepper(dve, S["dve_step"])
            key_part, lo_part = edge_rows_sb[:, :, 0], edge_rows_sb[:, :, 1]
            dve.wait_ge(S["dst_in"], 16)
            dst_v = dst_i[:].rearrange("p (c e) -> p c e", c=CPP)
            src_v = src_i[:].rearrange("p (c e) -> p c e", c=CPP)
            dve.tensor_reduce(spans[:, 0], dst_v, AX.X, ALU.min)
            dve.tensor_reduce(spans[:, 1], dst_v, AX.X, ALU.max).then_inc(S["spans_ready"], 1)
            dve.wait_ge(S["src_in"], 16)
            step(dve.tensor_scalar(lo_part, src_v, 1.0 / T, 0.5 / T - 0.5, ALU.mult, ALU.add))
            step(dve.tensor_scalar(lo_part, lo_part, ROUND, ROUND, ALU.add, ALU.subtract))
            step(dve.scalar_tensor_tensor(edge_a[:], lo_part, -float(T), src_v, ALU.mult, ALU.add))
            dve.scalar_tensor_tensor(key_part, dst_v, float(T), edge_a[:], ALU.mult, ALU.add).then_inc(S["keys_ready"], 1)

            def normalise(t):
                dve.wait_ge(x_in_sems[t % 4], 16 * (t // 4 + 1))
                step(dve.bn_stats(stat1[:, t], x_in[:, t % 4]))
                dve.bn_aggr(mv1[:, t], stat1[:, t]).then_inc(S["stats_ready"], 1)

            def normalise_end(t):
                dve.wait_ge(S["std_ready"], t + 1)
                step(dve.reciprocal(rstd1[:, t:t + 1], std1[:, t:t + 1]))
                if t >= 2:
                    dve.wait_ge(S["xn_lo_ready"], t - 1)
                ins = dve.tensor_scalar(xn[:, t % 2], x_in[:, t % 4], mv1[:, t, 0:1], rstd1[:, t:t + 1],
                                        ALU.subtract, ALU.mult)
                ins.then_inc(S["xn_ready"], 1)

            def find_windows():
                dve.wait_ge(S["tables"], 1)
                dve.wait_ge(S["spans_in"], 16)
                for a in range(2):
                    step(dve.tensor_scalar(hit[:, a], spans_b[:, 1], win_lo[:, a:a + 1], None, ALU.is_lt, ALU.add,
                                           accum_out=first[:, a:a + 1]))
                for a in range(2):
                    ins = dve.tensor_scalar(slot_i[:, a], slot_iota[:], first[:, a:a + 1], None, ALU.add)
                ins.then_inc(S["idx_ready"], 1)
                for a in range(2):
                    step(dve.tensor_scalar(hit[:, a], spans_b[:, 0], win_hi[:, a:a + 1], None, ALU.is_le, ALU.add,
                                           accum_out=last[:, a:a + 1]))
                step(dve.scalar_tensor_tensor(flaw[:, 0:2], first[:], float(KS), last[:], ALU.add, ALU.is_lt))
                dve.wait_ge(S["next_in"], 64)
                for n, op in enumerate((ALU.is_gt, ALU.is_equal)):
                    step(dve.tensor_tensor(edge_a[:].rearrange("p c e -> p (c e)"), dst_i[:], dst_next[:, n], op))
                    step(dve.tensor_reduce(flaw[:, n + 2:n + 3], edge_a[:], AX.XY, ALU.max))
                step(dve.tensor_reduce(flaw[:, 4:5], flaw[:, 0:4], AX.X, ALU.add))
                dve.tensor_copy(flaw[:, 0:1], flaw[:, 4:5]).then_inc(S["flaws_ready"], 1)

            def take_rows(k):
                at = 256 * (k % 2)
                dve.tensor_tensor(key_w[:, :, k], psum[:, AGG + k // 2, at:at + NW], win_base[:, k // KS], ALU.subtract)
                dve.tensor_copy(lo_w[:, :, k], psum[:, AGG + k // 2, at + 128:at + 128 + NW]).then_inc(S["rows_used"], 1)

            for t in range(T):
                normalise(t)
                if t >= 1:
                    normalise_end(t - 1)
                if t == LOOK:
                    find_windows()
            normalise_end(T - 1)
            dve.wait_ge(S["tables"], 2)
            dve.wait_ge(S["rows_turned"], SL)
            for k in range(SL):
                take_rows(k)
            dve.wait_ge(S["rows_used"], SL)
            dve.wait_ge(S["flaws_done"], 1)
            dve.tensor_scalar(flag_i[:], psum[0:1, SM, 0:1], 1.0, None, ALU.min).then_inc(S["range_ready"], 2)

            dve.wait_ge(S["range_in"], 16)
            flag = dve.value_load(range_row[0:1, 2 * NW:], min_val=0, max_val=1)
            with dve.If(flag > 0):
                bounds = stepper(dve, S["bounds_step"])
                bounds(dve.tensor_scalar(hit[:, 0], spans_b[:, 0], win_hi[:, 1:2], None, ALU.is_le))
                bounds(dve.scalar_tensor_tensor(hit[:, 0], spans_b[:, 1], win_lo[:, 0:1], hit[:, 0], ALU.is_ge, ALU.mult))
                for n, places in enumerate((chunk_down, chunk_up)):
                    bounds(dve.tensor_tensor(hit[:, 1], hit[:, 0], places[:], ALU.mult))
                    bounds(dve.tensor_reduce(whole[:, n:n + 1], hit[:, 1], AX.X, ALU.max))
                bounds(dve.tensor_scalar(whole[:, 0:1], whole[:, 0:1], -1.0, float(NCH), ALU.mult, ALU.add))
                bounds(dve.tensor_copy(span_i[:, 0:1], whole[:, 0:1]))
                dve.scalar_tensor_tensor(span_i[:, 1:2], whole[:, 0:1], 1.0, whole[:, 1:2], ALU.add, ALU.max)\
                   .then_inc(S["bounds_ready"], 1)
                dve.wait_ge(S["bounds_in"], 16)
                dve.memset(key_all[:], FAR)
                dve.memset(lo_all[:], -1.0).then_inc(S["gen_cleared"], 1)
                dve.wait_ge(S["gen_cleared"], 1)
                dve.wait_ge(S["gen_turned"], 1)
                for n, (table, j) in enumerate((table, j) for table in (key_all, lo_all) for j in range(CPP)):
                    place = table[:, 0:NCH].rearrange("p (c j) -> p j c", j=CPP)[:, j]
                    dve.tensor_copy(place, psum[:, AGG + n // 4, 128 * (n % 4):128 * (n % 4) + P]).then_inc(S["gen_taken"], 1)
                dve.wait_ge(S["gen_taken"], 2 * CPP)
                visit = dve.alloc_register("dve_visit")
                dve.reg_mov(visit, 0)
                with dve.Fori(0, NW) as w:
                    start = dve.value_load(range_row[0:1, bass.ds(w * 2, 1)], min_val=0, max_val=NCH)
                    end = dve.value_load(range_row[0:1, bass.ds(w * 2 + 1, 1)], min_val=1, max_val=NCH + 1)
                    with dve.Fori(start, end) as c:
                        n = dve.snap(visit, min_val=0, max_val=NW * NCH)
                        dve.wait_ge(S["gen_free"], n + 1)
                        dve.tensor_scalar(gen_key[:], gen_iota[:], win_base[:, 0, bass.ds(w, 1)], key_all[:, bass.ds(c, 1)],
                                          ALU.add, ALU.is_equal)
                        dve.tensor_scalar(gen_lo[:], iota_lo[:, :, 0], lo_all[:, bass.ds(c, 1)], None, ALU.is_equal)\
                           .then_inc(S["gen_ready"], 1)
                        dve.reg_add(visit, visit, 1)
                    dve.wait_ge(S["gen_win"], w + 1)
                    dve.wait_ge(S["gen_stored"], w + 1)
                    window_sum = psum[:, WIN, 0:MW].rearrange("p (w h) -> p h w", w=W)
                    dve.tensor_copy(gen_counts[:, 0], window_sum).then_inc(S["gen_half"], 1)
                    dve.wait_ge(S["gen_half"], w + 1)
                    dve.tensor_tensor(gen_counts[:, 1], window_sum, gen_counts[:, 0], ALU.subtract).then_inc(S["gen_split"], 1)
                dve.wait_ge(S["gen_stored"], NW + 1)

            def one_hots(w):
                if w >= RING:
                    dve.wait_ge(S["win_done"], w - RING + 1)
                for hot, iota, value, width in ((hot_key, iota_key, key_w, MH), (hot_lo, iota_lo, lo_w, 128)):
                    ins = dve.tensor_tensor(hot[:, w % RING],
                                            iota[:].rearrange("p (a n) k -> p a n k", a=1).broadcast_to([128, 2, width, KS]),
                                            value[:, w].rearrange("p (a n k) -> p a n k", a=2, n=1)
                                            .broadcast_to([128, 2, width, KS]), ALU.is_equal)
                ins.then_inc(S["hot_ready"], 1)

            def split_sums(g):
                if g == 0:
                    dve.wait_ge(S["w_split"], 2)
                for c in range(KC):
                    dve.wait_ge(S["hT_hi_ready"], 4 * g + c + 1)
                    dve.tensor_tensor(hT_lo[:, c], psum[:, AGG + c, 0:GN], hT_hi[:, c].bitcast(F32), ALU.subtract)\
                       .then_inc(S["hT_ready"], 1)

            def residual(g, q):
                n = 4 * g + q
                dve.wait_ge(S["mlp2_done"], n + 1)
                dve.wait_ge(S["res_sum"], n + 1)
                if n >= 2:
                    dve.wait_ge(x2_out[q % 2], 32 * (2 * g + q // 2))
                step(dve.tensor_tensor(x2[:, q % 2], psum[0:P, SM + q % 2, :], x_res[:, q % 2], ALU.add))
                step(dve.bn_stats(ln2[:, q % 2, 0:6], x2[:, q % 2]))
                dve.bn_aggr(ln2[:, q % 2, 6:8], ln2[:, q % 2, 0:6]).then_inc(S["x2_ready"], 1)

            def residual_end(g, q):
                n = 4 * g + q
                dve.wait_ge(S["std2_ready"], n + 1)
                if g >= 1:
                    dve.wait_ge(S["xt_turned"], n - 3)
                step(dve.reciprocal(ln2[:, q % 2, 9:10], ln2[:, q % 2, 8:9]))
                dve.tensor_scalar(xt[:, q], x2[:, q % 2], ln2[:, q % 2, 6:7], ln2[:, q % 2, 9:10],
                                  ALU.subtract, ALU.mult).then_inc(S["xt_ready"], 1)

            def gate_take(g, tiles):
                for q in tiles:
                    n = 4 * g + q
                    dve.wait_ge(S["gate_done"], n + 1)
                    dve.tensor_copy(logits[:, n], psum[0:P, SM + q % 2, 0:NE]).then_inc(S["gate_taken"], 1)
                for q in tiles:
                    n = 4 * g + q
                    dve.wait_ge(S["gate_taken"], n + 1)
                    dve.max(top[:, n], logits[:, n]).then_inc(S["top_ready"], 1)
                for q in tiles:
                    n = 4 * g + q
                    dve.wait_ge(S["top_ready"], n + 1)
                    dve.max_index(topi[:, n], top[:, n], logits[:, n]).then_inc(S["topi_ready"], 1)

            for it in range(G + 3):
                g = it - 2
                for part in range(PARTS):
                    for j in range(WP):
                        if it < G:
                            one_hots(WG * it + WP * part + j)
                        if 0 <= it - 3 and (part, j) == (3, 3):
                            gate_take(it - 3, (0, 1))
                        if 0 <= it - 3 and (part, j) == (4, 2):
                            gate_take(it - 3, (2, 3))
                        if j == RING - 1:
                            if part == 0:
                                if 0 <= g < G:
                                    split_sums(g)
                                if 0 <= g - 1 < G:
                                    for q in (2, 3):
                                        residual(g - 1, q)
                                    for q in (2, 3):
                                        residual_end(g - 1, q)
                            elif 0 <= g < G and part == 4:
                                for q in (0, 1):
                                    residual(g, q)
                                for q in (0, 1):
                                    residual_end(g, q)

            def over(ap, shape):
                return ap.broadcast_to(shape)

            dve.wait_ge(S["x2_landed"], 1)
            dve.wait_ge(S["topi_ready"], T)
            step(dve.tensor_copy(topf[:], topi[:, :, 0:2].rearrange("p n c -> p c n")))
            experts = iota_e[:].rearrange("p (o e) -> p o e", o=1).broadcast_to([P, T, NE])
            for c in range(2):
                ins = dve.tensor_tensor(chosen[:, c], experts, topf[:, c].rearrange("p (n o) -> p n o", o=1).broadcast_to([P, T, NE]),
                                        ALU.is_equal)
            step(ins)
            dve.tensor_tensor(either[:], chosen[:, 0], chosen[:, 1], ALU.add).then_inc(S["chosen_ready"], 1)
            dve.tensor_tensor(shifted[:], logits[:], top[:, :, 0:1].broadcast_to([P, T, NE]), ALU.subtract)
            dve.tensor_tensor(share[:], top[:, :, 0:2].rearrange("p n c -> p c n"),
                              top[:, :, 0:1].rearrange("p n o -> p o n").broadcast_to([P, 2, T]), ALU.subtract)\
               .then_inc(S["shifted_ready"], 1)
            dve.wait_ge(S["ranked"], 1)
            step(dve.tensor_copy(tile_count[:], psum[0:P, 1, 0:T * NE].rearrange("p (n e) -> p e n", e=NE)))
            dve.wait_ge(S["route_tables"], 1)
            step(dve.tensor_tensor_scan(count_up[:].rearrange("p e n -> p (e n)"), goes_on[:].rearrange("p e n -> p (e n)"),
                                        tile_count[:].rearrange("p e n -> p (e n)"), 0.0, ALU.mult, ALU.add))
            dve.tensor_tensor(slot_of[:], count_up[:], tile_count[:], ALU.subtract)
            step(dve.tensor_scalar(blocks[:], count_up[:, :, T - 1], 1.0 / B, (B - 1.0) / B - 0.5 + 0.5 / B, ALU.mult, ALU.add))
            step(dve.tensor_scalar(blocks[:], blocks[:], ROUND, ROUND, ALU.add, ALU.subtract))
            step(dve.tensor_scalar(blocks[:], blocks[:], 1.0, None, ALU.max))
            step(dve.tensor_tensor_scan(block_end[:], ones[:].broadcast_to([P, NE]), blocks[:], 0.0, ALU.mult, ALU.add))
            step(dve.tensor_tensor(block_base[:], block_end[:], blocks[:], ALU.subtract))
            step(dve.tensor_tensor(slot_of[:], slot_of[:], psum[0:P, 0, 0:T * NE].rearrange("p (n e) -> p e n", e=NE), ALU.add))
            step(dve.scalar_tensor_tensor(slot_of[:], block_base[:].rearrange("p (e o) -> p e o", o=1).broadcast_to([P, NE, T]),
                                          float(B), slot_of[:], ALU.mult, ALU.add))
            for c in range(2):
                ins = dve.tensor_tensor(picked[:, c], chosen[:, c], slot_of[:].rearrange("p e n -> p n e"), ALU.mult)
            step(ins)
            step(dve.tensor_reduce(dest[:], picked[:].rearrange("p c n e -> p (c n) e"), AX.X, ALU.add))
            step(dve.tensor_scalar(dest_tile[:], dest[:], 1.0 / 128, -0.5 + 0.5 / 128, ALU.mult, ALU.add))
            step(dve.tensor_scalar(dest_tile[:], dest_tile[:], ROUND, ROUND, ALU.add, ALU.subtract))
            dve.tensor_copy(dest_tile16[:], dest_tile[:])
            step(dve.scalar_tensor_tensor(dest_row[:], dest_tile[:], -128.0, dest[:], ALU.mult, ALU.add))
            (dve.tensor_tensor(at_tile[:], iota_nt[:].rearrange("p (o s) -> p o s", o=1).broadcast_to([P, 2 * T, NT]),
                                   dest_tile16[:].rearrange("p (n o) -> p n o", o=1).broadcast_to([P, 2 * T, NT]), ALU.is_equal)
                 .then_inc(S["at_tile_ready"], 1))
            dve.wait_ge(S["at_tile_ready"], 1)
            dve.tensor_tensor(token_part[:, :, 1], at_tile[:],
                              iota_n[:].rearrange("p c (n o) -> p (c n) o", o=1).broadcast_to([P, 2 * T, NT]), ALU.mult)\
               .then_inc(S["parts_ready"], 1)
            for n in range(0, 2 * T, SPREAD):
                dve.tensor_tensor(at_row[:, n:n + SPREAD], iota_128[:].rearrange("p (o s) -> p o s", o=1).broadcast_to([P, SPREAD, 128]),
                                  dest_row[:, n:n + SPREAD].rearrange("p (n o) -> p n o", o=1).broadcast_to([P, SPREAD, 128]),
                                  ALU.is_equal).then_inc(S["spread_ready"], 1)
            step(dve.tensor_tensor(ends_before[:], block_end[0:1].rearrange("p (o e) -> p o e", o=1).broadcast_to([1, NB, NE]),
                                   iota_k[:].rearrange("p (k o) -> p k o", o=1).broadcast_to([1, NB, NE]), ALU.is_le))
            step(dve.tensor_reduce(expert_f[:], ends_before[:], AX.X, ALU.add))
            dve.tensor_scalar(expert_i[:], expert_f[:], float(NE - 1), None, ALU.min)
            dve.tensor_copy(end_i[:], block_end[0:1]).then_inc(S["slots_known"], 1)
            dve.wait_ge(S["spread_done"], 1)
            step(dve.tensor_copy(dest_i[:], dest[:]))
            step(dve.tensor_copy(token_low[:], psum[:, 2, 0:NT]))
            dve.scalar_tensor_tensor(token_i[:], psum[:, 2, NT:2 * NT], float(P), token_low[:], ALU.mult, ALU.add)\
               .then_inc(S["tokens_ready"], 1)
            dve.wait_ge(S["exp_ready"], 1)
            step(dve.tensor_reduce(total[:], shifted[:], AX.X, ALU.add))
            step(dve.reciprocal(total[:], total[:]))
            step(dve.tensor_tensor(share[:], share[:], total[:].rearrange("p (o n) -> p o n", o=1).broadcast_to([P, 2, T]), ALU.mult))
            step(dve.tensor_tensor(share_sum[:], share[:, 0], share[:, 1], ALU.add))
            step(dve.tensor_scalar(share_sum[:], share_sum[:], 1e-6, None, ALU.add))
            step(dve.reciprocal(share_sum[:], share_sum[:]))
            step(dve.tensor_tensor(share[:], share[:], share_sum[:].rearrange("p (o n) -> p o n", o=1).broadcast_to([P, 2, T]), ALU.mult))
            for c in range(2):
                ins = dve.tensor_tensor(chosen[:, c], chosen[:, c], share[:, c].rearrange("p (n o) -> p n o", o=1).broadcast_to([P, T, NE]),
                                        ALU.mult)
            step(ins)
            dve.tensor_tensor(scores[:], chosen[:, 0], chosen[:, 1], ALU.add).then_inc(S["scores_ready"], 1)
            for n in range(0, T, 4):
                dve.wait_ge(S["scores_turned"], n // 4 + 1)
                dve.tensor_copy(scores_T[:, n:n + 4], psum[0:NE, 3 + n // 4, 0:4 * P].rearrange("p (q n) -> p q n", q=4))\
                   .then_inc(S["scores_T_ready"], 1)

            def turned_low(k):
                for i in range(2):
                    dve.wait_ge(S["xT_hi_ready"], 2 * k + i + 1)
                    part = slice(i * 128, (i + 1) * 128)
                    dve.tensor_tensor(xT_lo[:, :, part], psum[:, i].rearrange("p (c n) -> p c n", c=KC),
                                      xT_hi[:, :, part].bitcast(F32), ALU.subtract).then_inc(S["xT_ready"], 1)

            turned_low(0)
            dve.sem_inc(S["y0_taken"], 1)
            for k in range(NB):
                for m in range(HC):
                    dve.wait_ge(S["gelu_ready"], HC * k + m + 1)
                    if k >= 1:
                        dve.wait_ge(S["down_done"], 2 * k)
                    step(dve.tensor_copy(he_hi[:, m], he[:, m]))
                    dve.tensor_tensor(he_lo[:, m], he[:, m], he_hi[:, m].bitcast(F32), ALU.subtract).then_inc(S["he_ready"], 1)
                turned_low(k + 1)
                dve.wait_ge(S["down_done"], 2 * k + 1)
                if k >= 2:
                    dve.wait_ge(y_out[k % 2], 16 * (k // 2))
                dve.tensor_copy(y[:, k % 2, 0], psum[:, 4]).then_inc(S["y0_taken"], 1)

            def add_bias(n):
                dve.wait_ge(S["bias_done"], n + 1)
                dve.tensor_tensor(x2_back[:, n], x2_back[:, n], psum[0:P, 1 + n % 4, :], ALU.add).then_inc(S["bias_added"], 1)

            dve.wait_ge(S["x2_back_in"], 16 * (T // 4))
            for n in range(4):
                add_bias(n)
            for n in range(T):
                row = x2_back[:, n]
                dve.wait_ge(S["bias_added"], n + 1)
                dve.wait_ge(yb_in[n % 4], 32 * (n // 4 + 1))
                step(dve.scalar_tensor_tensor(row, y_back[:, n % 4, 0], share[:, 0, n:n + 1], row, ALU.mult, ALU.add))
                dve.scalar_tensor_tensor(row, y_back[:, n % 4, 1], share[:, 1, n:n + 1], row, ALU.mult, ALU.add)\
                   .then_inc(S["summed"], 1)
                if n + 4 < T:
                    add_bias(n + 4)

        @block.tensor
        def _(pe):
            mm = pe.matmul
            pe.wait_ge(S["tables"], 2)
            pe.wait_ge(S["gathered"], 16 * SL)
            for k in range(SL):
                at = 256 * (k % 2)
                pe.transpose(psum[:, AGG + k // 2, at:at + NW], slot_rows[:, k, 0:CH], ident[0:NW, 0:NW])
                pe.transpose(psum[:, AGG + k // 2, at + 128:at + 128 + NW], slot_rows[:, k, CH:2 * CH], ident[0:NW, 0:NW])\
                  .then_inc(S["rows_turned"], 1)

            pe.wait_ge(S["flaws_ready"], 1)
            mm(psum[0:1, SM, 0:1], flaw[:, 0:1], ones[:], start=True, stop=True).then_inc(S["flaws_done"], 1)
            pe.wait_ge(S["range_in"], 16)
            flag = pe.value_load(range_row[0:1, 2 * NW:], min_val=0, max_val=1)
            with pe.If(flag > 0):
                pe.wait_ge(S["rows_used"], SL)
                for n, (v, j) in enumerate((v, j) for v in range(2) for j in range(CPP)):
                    ins = pe.transpose(psum[:, AGG + n // 4, 128 * (n % 4):128 * (n % 4) + P], edge_rows_sb[:, j, v], ident[0:P, 0:P])
                ins.then_inc(S["gen_turned"], 1)
                pe.sem_inc(S["gen_free"], 1)
                visit = pe.alloc_register("pe_visit")
                pe.reg_mov(visit, 0)
                bank = psum[:, WIN, 0:MW]
                pe.wait_ge(S["bounds_in"], 16)
                with pe.Fori(0, NW) as w:
                    start = pe.value_load(range_row[0:1, bass.ds(w * 2, 1)], min_val=0, max_val=NCH)
                    end = pe.value_load(range_row[0:1, bass.ds(w * 2 + 1, 1)], min_val=1, max_val=NCH + 1)
                    pe.wait_ge(S["gen_stored"], w + 1)
                    mm(bank, self_row[:, bass.ds(w * -1 + 127, 128)], self_cols[:], start=True, stop=False)
                    with pe.Fori(start, end) as c:
                        n = pe.snap(visit, min_val=0, max_val=NW * NCH)
                        pe.wait_ge(S["gen_ready"], n + 1)
                        mm(bank, gen_lo[:], gen_key[:], start=False, stop=False).then_inc(S["gen_free"], 1)
                        pe.reg_add(visit, visit, 1)
                    mm(psum[0:127, WIN, 0:MW], self_row[:, 128:255], self_cols[:], start=False, stop=True)\
                      .then_inc(S["gen_win"], 1)

            def window(w, j):
                free = {0: w, 1: w - 1}.get(j, w - 1)
                if free > 0:
                    pe.wait_ge(S["counts_ready"], free)
                pe.wait_ge(S["hot_ready"], w + 1)
                for a in range(2):
                    half = psum[:, WIN + j % 2, a * MH:(a + 1) * MH]
                    mm(half, self_row[:, 127 - w:255 - w], self_cols[:, a * MH:(a + 1) * MH], start=True, stop=False)
                    for k in range(KS):
                        ins = mm(half, hot_lo[:, w % RING, a, :, k], hot_key[:, w % RING, a, :, k], start=False, stop=(k == KS - 1))
                ins.then_inc(S["win_done"], 1)

            def sums(g, part):
                if part == 0:
                    pe.wait_ge(S["counts_final"], g + 1)
                    if g >= 1:
                        pe.wait_ge(S["hT_ready"], 4 * g)
                for t in range(TP * part, TP * part + TP):
                    if g == 0:
                        pe.wait_ge(S["xn_hi_ready"], t + 1)
                        pe.wait_ge(S["xn_lo_ready"], t + 1)
                    for n, half in enumerate((xn_hi, xn_lo)):
                        for c in range(KC):
                            ins = mm(psum[:, AGG + c, 0:GN], half[:, t, c * 128:(c + 1) * 128], counts[0:P, g % 2, t],
                                     start=(t == 0 and n == 0), stop=(t == T - 1 and n == 1))
                if part == PARTS - 1:
                    ins.then_inc(S["agg_main"], 1)
                    with pe.If(flag > 0):
                        pe.wait_ge(S["rest_in"], 16 * (g + 1))
                        for t in range(T):
                            for half in (xn_hi, xn_lo):
                                for c in range(KC):
                                    mm(psum[:, AGG + c, 0:GN], half[:, t, c * 128:(c + 1) * 128], counts[0:P, g % 2, t],
                                       start=False, stop=(t == T - 1 and half is xn_lo), skip_group_check=True)
                    mm(psum[0:127, AGG + KC - 1, 0:MW], self_row[:, 128:255], self_cols[:], start=False, stop=True,
                       skip_group_check=True).then_inc(S["agg_done"], 1)

            def mlp1(g, m):
                if m == 0:
                    pe.wait_ge(S["hT_ready"], 4 * (g + 1))
                    pe.wait_ge(S["w_split"], 1)
                if m >= 2:
                    pe.wait_ge(S["relu_ready"], 4 * g + m - 1)
                elif g >= 1:
                    pe.wait_ge(S["x2_ready"], 4 * g + m - 1)
                cols = slice(m * 128, (m + 1) * 128)
                trio = [(W1_hi, hT_hi), (W1_lo, hT_hi), (W1_hi, hT_lo)]
                for k in range(KC):
                    for n, (w_, h_) in enumerate(trio):
                        ins = mm(psum[:, SM + m % 2, 0:GN], w_[:, k, cols], h_[:, k], start=(k == 0 and n == 0),
                                 stop=(k == KC - 1 and n == 2))
                ins.then_inc(S["mlp1_done"], 1)

            def mlp2(g, q):
                if q == 0:
                    pe.wait_ge(S["h1_split"], 4 * (g + 1))
                    pe.wait_ge(S["w_split"], 2)
                if q >= 2:
                    pe.wait_ge(S["x2_ready"], 4 * g + q - 1)
                elif g >= 1:
                    pe.wait_ge(S["gate_taken"], 4 * (g - 1) + q + 3)
                rows = slice(q * P, (q + 1) * P)
                trio = [(h1_hi, W2_hi), (h1_hi, W2_lo), (h1_lo, W2_hi)]
                for k in range(KC):
                    for n, (h_, w_) in enumerate(trio):
                        ins = mm(psum[0:P, SM + q % 2, :], h_[:, k, rows], w_[:, k], start=(k == 0 and n == 0),
                                 stop=(k == KC - 1 and n == 2))
                ins.then_inc(S["mlp2_done"], 1)

            def gate_turn(g, tiles):
                for q in tiles:
                    n = 4 * g + q
                    pe.wait_ge(S["xt_ready"], n + 1)
                    if q >= 2:
                        pe.wait_ge(S["gate_taken"], n - 1)
                    elif g + 1 < G:
                        pe.wait_ge(S["relu_ready"], 4 * (g + 1) + q + 3)
                    elif g + 1 == G:
                        pe.wait_ge(S["x2_ready"], 4 * G)
                    for c in range(KC):
                        ins = pe.transpose(psum[:, SM + q % 2, c * P:(c + 1) * P], xt[:, q, c * 128:(c + 1) * 128], ident[0:P, 0:P])
                    ins.then_inc(S["xt_turned"], 1)

            def gate(g, tiles):
                for q in tiles:
                    n = 4 * g + q
                    pe.wait_ge(S["xt_T_ready"], n + 1)
                    for c in range(KC):
                        ins = mm(psum[0:P, SM + q % 2, 0:NE], h1[:, q % 2, c * P:(c + 1) * P], Wg_sb[:, c],
                                 start=(c == 0), stop=(c == KC - 1))
                    ins.then_inc(S["gate_done"], 1)

            pe.wait_ge(S["small_in"], 48)
            for it in range(G + 3):
                for part in range(PARTS):
                    for j in range(WP):
                        if it < G:
                            window(WG * it + WP * part + j, j)
                        if 0 <= it - 3:
                            if (part, j) == (2, 2):
                                gate_turn(it - 3, (0, 1))
                            if (part, j) == (3, 0):
                                gate_turn(it - 3, (2, 3))
                            if (part, j) == (3, 3):
                                gate(it - 3, (2, 3))
                    if 0 <= it - 1 < G:
                        sums(it - 1, part)
                    if 0 <= it - 2 < G:
                        for m in mlp1_chunks(part):
                            mlp1(it - 2, m)
                        for q in mlp2_tiles(part):
                            mlp2(it - 2, q)
                    if 0 <= it - 3 and part == 2:
                        gate(it - 3, (0, 1))

            pe.wait_ge(S["chosen_ready"], 1)
            pe.wait_ge(S["route_tables"], 1)
            choices = either[:].rearrange("p n e -> p (n e)")
            mm(psum[0:P, 0, 0:T * NE], before[:], choices, start=True, stop=True)
            mm(psum[0:P, 1, 0:T * NE], ones16[:], choices, start=True, stop=True).then_inc(S["ranked"], 1)
            pe.wait_ge(S["parts_ready"], 2)
            for n in range(2 * T):
                if n % SPREAD == 0:
                    pe.wait_ge(S["spread_ready"], n // SPREAD + 1)
                ins = mm(psum[:, 2, 0:2 * NT], at_row[:, n], token_part[:, n].rearrange("p a s -> p (a s)"),
                         start=(n == 0), stop=(n == 2 * T - 1))
            ins.then_inc(S["spread_done"], 1)

            def turn(k):
                pe.wait_ge(S["x_now_ready"], k + 1)
                for i in range(2):
                    for c in range(KC):
                        ins = pe.transpose(psum[:, i, c * 128:(c + 1) * 128], x_now[:, i, c * 128:(c + 1) * 128], ident[:])
                    ins.then_inc(S["turned"], 1)

            pe.wait_ge(S["scores_ready"], 1)
            for n in range(T):
                ins = pe.transpose(psum[0:NE, 3 + n // 4, n % 4 * P:(n % 4 + 1) * P], scores[:, n], ident[0:P, 0:P])
                if n % 4 == 3:
                    ins.then_inc(S["scores_turned"], 1)
            turn(0)
            pe.wait_ge(S["scores_T_ready"], T // 4)
            pe.wait_ge(S["tokens_ready"], 1)
            pe.wait_ge(S["slots_known"], 1)
            start = 0
            for e in range(NE):
                end = pe.value_load(end_i[0:1, e:e + 1], min_val=1, max_val=NB)
                pe.wait_ge(S["w_lo_ready"], e + 1)
                with pe.Fori(start, end) as k:
                    pe.wait_ge(S["xT_ready"], k * 2 + 2)
                    trio = [(w1_hi, xT_hi), (w1_lo, xT_hi), (w1_hi, xT_lo)]
                    for m in range(HC):
                        cols = slice(m * 128, (m + 1) * 128)
                        for c in range(KC):
                            for i, (w_, x_) in enumerate(trio):
                                ins = mm(psum[:, 2 + m, 0:B], w_[e][:, c, cols], x_[:, c], start=(c == 0 and i == 0),
                                         stop=(c == KC - 1 and i == 2))
                        ins.then_inc(S["up_done"], 1)
                    turn(k + 1)
                    trio = [(he_hi, w2_hi), (he_hi, w2_lo), (he_lo, w2_hi)]
                    for m in range(HC):
                        pe.wait_ge(S["he_ready"], k * 2 + (m + 1))
                        for i in range(2):
                            if m == 0:
                                pe.wait_ge((S["y0_taken"], S["y1_taken"])[i], k + 1)
                            for n, (h_, w_) in enumerate(trio):
                                ins = mm(psum[:, 4 + i, :], h_[:, m, i * 128:(i + 1) * 128], w_[e][:, m],
                                         start=(m == 0 and n == 0), stop=(m == HC - 1 and n == 2))
                            if m == HC - 1:
                                ins.then_inc(S["down_done"], 1)
                start = end
            with pe.If(start < NB):
                with pe.Fori(start, NB) as k:
                    pe.wait_ge(S["xT_ready"], k * 2 + 2)
                    pe.sem_inc(S["up_done"], HC)
                    pe.wait_ge(S["x_now_ready"], k + 2)
                    pe.sem_inc(S["turned"], 2)
                    pe.wait_ge(S["he_ready"], k * 2 + HC)
                    for i in range(2):
                        pe.wait_ge((S["y0_taken"], S["y1_taken"])[i], k + 1)
                    pe.sem_inc(S["down_done"], 2)

            pe.wait_ge(S["eb_in"], 32)
            pe.wait_ge(S["y0_taken"], NB + 1)
            pe.wait_ge(S["y1_taken"], NB + 1)
            for n in range(T):
                if n >= 4:
                    pe.wait_ge(S["bias_added"], n - 3)
                mm(psum[0:P, 1 + n % 4, :], scores_T[:, n], eb2_sb[:], start=True, stop=True).then_inc(S["bias_done"], 1)


_INS = ["x", "src", "dst", "L0_gnn_W1", "L0_gnn_b1", "L0_gnn_W2", "L0_gnn_b2",
        "L0_ffn_Wg", "L0_ffn_W1", "L0_ffn_b1", "L0_ffn_W2", "L0_ffn_b2"]


def kernel(**inputs):
    import numpy as _np
    import concourse.bacc as _bacc
    from concourse.bass_utils import run_bass_kernel_spmd as _run

    nc = _bacc.Bacc("TRN2", target_bir_lowering=False, num_devices=1)
    arrays, args = {}, []
    for name in _INS:
        a = _np.ascontiguousarray(inputs[name])
        arrays[f"in_{name}"] = a
        args.append(nc.dram_tensor(f"in_{name}", a.shape, mybir.dt.from_np(a.dtype), kind="ExternalInput").ap())
    args.append(nc.dram_tensor("out_x", (N, D), F32, kind="ExternalOutput").ap())
    gnn_moe(nc, *args)
    r = _run(nc, [arrays], core_ids=[0])
    return r.results[0]["out_x"]
```
